# Optimizing a Trainium2 kernel written in Bass

```python
import numpy as np
import jax
import jax.numpy as jnp

def _softmax(x, axis=-1):
    return jax.nn.softmax(x, axis=axis)

def _gelu(x):
    return jax.nn.gelu(x, approximate=True)

def _silu(x):
    return jax.nn.silu(x)

def _sigmoid(x):
    return jax.nn.sigmoid(x)

def _layernorm(x, axis=-1, eps=1e-05):
    m = jnp.mean(x, axis=axis, keepdims=True)
    v = jnp.var(x, axis=axis, keepdims=True)
    return (x - m) / jnp.sqrt(v + eps)

def _scatter_add(tgt, idx, src, axis=0):
    return tgt.at[idx].add(src)

def _segment_sum(src, seg, n):
    return jax.ops.segment_sum(src, seg, n)
kernel_name = 'mk_macaron_d1_jaxref_r8_e16eb8'

def setup_inputs(seed: int=0):
    np.random.seed(seed)
    _w = jnp.asarray

    def _L0_attn_setup():
        import jax, jax.numpy as jnp
        import numpy as np
        B, S, E, H, G = (2, 256, 256, 16, 4)
        D = E // H
        key = jax.random.key(seed)
        ks = jax.random.split(key, 7)
        scale = 1.0 / np.sqrt(E)
        x = jax.random.normal(ks[0], (B, S, E), dtype=jnp.float32)
        Wq = jax.random.normal(ks[1], (H, E, D), dtype=jnp.float32) * scale
        bq = jax.random.normal(ks[2], (H, D), dtype=jnp.float32) * 0.02
        Wk = jax.random.normal(ks[3], (G, E, D), dtype=jnp.float32) * scale
        bk = jax.random.normal(ks[4], (G, D), dtype=jnp.float32) * 0.02
        Wv = jax.random.normal(ks[5], (G, E, D), dtype=jnp.float32) * scale
        bv = jax.random.normal(ks[6], (G, D), dtype=jnp.float32) * 0.02
        return {'x': x, 'Wq': Wq, 'bq': bq, 'Wk': Wk, 'bk': bk, 'Wv': Wv, 'bv': bv}
    _L0_attn_in = _L0_attn_setup()

    def _L0_ffn_setup():
        import jax, jax.numpy as jnp
        import numpy as np
        D_MODEL = 256
        D_EXPERT = 1024
        EPS = 1e-08

        def ternary_quant(w):
            scale = jnp.mean(jnp.abs(w)) + EPS
            q = jnp.clip(jnp.round(w / scale), -1.0, 1.0) * scale
            return w + jax.lax.stop_gradient(q - w)
        key = jax.random.key(seed)
        k_x, k_up, k_gate, k_down = jax.random.split(key, 4)
        std_in = 1.0 / np.sqrt(D_MODEL)
        std_exp = 1.0 / np.sqrt(D_EXPERT)
        return {'x': jax.random.normal(k_x, (4, 256, D_MODEL), dtype=jnp.float32), 'W_up': jax.random.normal(k_up, (D_EXPERT, D_MODEL), dtype=jnp.float32) * std_in, 'W_gate': jax.random.normal(k_gate, (D_EXPERT, D_MODEL), dtype=jnp.float32) * std_in, 'W_down': jax.random.normal(k_down, (D_MODEL, D_EXPERT), dtype=jnp.float32) * std_exp}
    _L0_ffn_in = _L0_ffn_setup()
    _d = {'L0_attn_x': _L0_attn_in['x'], 'L0_attn_Wq': _L0_attn_in['Wq'], 'L0_attn_bq': _L0_attn_in['bq'], 'L0_attn_Wk': _L0_attn_in['Wk'], 'L0_attn_bk': _L0_attn_in['bk'], 'L0_attn_Wv': _L0_attn_in['Wv'], 'L0_attn_bv': _L0_attn_in['bv'], 'L0_ffn_W_up': _L0_ffn_in['W_up'], 'L0_ffn_W_gate': _L0_ffn_in['W_gate'], 'L0_ffn_W_down': _L0_ffn_in['W_down']}
    _x0 = _d['L0_attn_x']
    _d['L0_attn_x'] = jax.random.normal(jax.random.fold_in(jax.random.key(seed), 1), (16, 256, 256), dtype=_x0.dtype)
    del _x0
    return _d

def reference(L0_attn_x, L0_attn_Wq, L0_attn_bq, L0_attn_Wk, L0_attn_bk, L0_attn_Wv, L0_attn_bv, L0_ffn_W_up, L0_ffn_W_gate, L0_ffn_W_down):

    def _L0_attn_ref(x, Wq, bq, Wk, bk, Wv, bv):
        import jax, jax.numpy as jnp
        import numpy as np
        B, S, E, H, G = (2, 256, 256, 16, 4)
        D = E // H
        h, e, d = Wq.shape
        g = Wk.shape[0]
        per = h // g
        s = x.shape[1]
        q = jnp.einsum('bse,hed->bhsd', x, Wq) + bq[None, :, None, :]
        kg = jnp.einsum('bse,ged->bgsd', x, Wk) + bk[None, :, None, :]
        vg = jnp.einsum('bse,ged->bgsd', x, Wv) + bv[None, :, None, :]
        k = jnp.repeat(kg, per, axis=1)
        v = jnp.repeat(vg, per, axis=1)
        scores = jnp.einsum('bhqd,bhkd->bhqk', q, k) * (1.0 / np.sqrt(d))
        causal = jnp.triu(jnp.ones((s, s), dtype=bool), k=1)
        scores = jnp.where(causal[None, None, :, :], -jnp.inf, scores)
        attn = jax.nn.softmax(scores, axis=-1)
        out = jnp.einsum('bhqk,bhkd->bhqd', attn, v)
        return out.transpose(0, 2, 1, 3).reshape(x.shape[0], s, h * d)

    def _L0_ffn_ref(x, W_up, W_gate, W_down):
        import jax, jax.numpy as jnp
        import numpy as np
        D_MODEL = 256
        D_EXPERT = 1024
        EPS = 1e-08

        def ternary_quant(w):
            scale = jnp.mean(jnp.abs(w)) + EPS
            q = jnp.clip(jnp.round(w / scale), -1.0, 1.0) * scale
            return w + jax.lax.stop_gradient(q - w)
        wu = ternary_quant(W_up)
        wg = ternary_quant(W_gate)
        wd = ternary_quant(W_down)
        up = jnp.einsum('bsd,ed->bse', x, wu)
        gate = jnp.einsum('bsd,ed->bse', x, wg)
        hidden = jax.nn.silu(up) * gate
        return jnp.einsum('bse,de->bsd', hidden, wd)
    x = L0_attn_x
    x = x + 0.5 * _L0_ffn_ref(_layernorm(x, axis=-1), L0_ffn_W_up, L0_ffn_W_gate, L0_ffn_W_down)
    x = x + _L0_attn_ref(_layernorm(x, axis=-1), L0_attn_Wq, L0_attn_bq, L0_attn_Wk, L0_attn_bk, L0_attn_Wv, L0_attn_bv)
    x = x + 0.5 * _L0_ffn_ref(_layernorm(x, axis=-1), L0_ffn_W_up, L0_ffn_W_gate, L0_ffn_W_down)
    return x

_drawn_inputs = setup_inputs


def setup_inputs(seed=0):
    import zlib

    import numpy as np

    out = dict(_drawn_inputs(seed))
    spreads = {}
    factors = {'L0_attn_bq': 8.0, 'L0_attn_bk': 8.0}
    for name, (base, spread) in spreads.items():
        noise = np.random.default_rng([zlib.crc32(name.encode()), seed]).standard_normal(out[name].shape)
        drawn = base * np.exp(spread * noise) if base else spread * noise
        out[name] = jnp.asarray(drawn.astype(out[name].dtype))
    for name, factor in factors.items():
        out[name] = (out[name] * factor).astype(out[name].dtype)
    return out
```

```python
from contextlib import ExitStack

import concourse.bass as bass
from concourse import mybir

P = 128
ALU = mybir.AluOpType
ACT = mybir.ActivationFunctionType
AXX = mybir.AxisListType.X
F32 = mybir.dt.float32
F16 = mybir.dt.float16
U32 = mybir.dt.uint32
I32 = mybir.dt.int32
RMAX = bass.bass_isa.ReduceOp.max

LN_EPS = 1e-5
QUANT_EPS = 1e-8
MASKED = -1e30
QK_BOUND = 2048.0
MAX_UNIT = 4096.0
EXPONENT_BITS = 0x7F800000
RSQRT_GUESS = 0x5F3759DF
RSTD_STEPS = 12


def macaron_block(nc, x_in, Wq, bq, Wk, bk, Wv, bv, W_up, W_gate, W_down, out):
    NB, S, D = x_in.shape
    H, _, DH = Wq.shape
    G = Wk.shape[0]
    HPG = H // G
    F = W_up.shape[0]
    ND = D // P
    NE = F // P
    TC = 512
    TT = TC // P
    NC = NB * S // TC
    BC = TC // S
    QT = S // P
    NT = NC * TT
    HH = H // 2
    VW = 32
    assert (ND, NE, TT, BC, QT, HPG, DH) == (2, 8, 4, 2, 2, 4, 16)

    x_dram = x_in.rearrange("b (t p) d -> p (b t) d", p=P)
    out_dram = out.rearrange("b (t p) d -> p (b t) d", p=P)
    q_scr = nc.dram_tensor("q_scratch", (2, 2, H, DH, TC), F16)
    k_scr = nc.dram_tensor("k_scratch", (2, 2, G, DH, TC), F16)

    with ExitStack() as ctx:
        def sb(name, shape, dt=F32):
            return ctx.enter_context(nc.sbuf_tensor(name, shape, dt))

        def sem(name):
            return ctx.enter_context(nc.semaphore(name))

        ident32 = sb("ident32", [P, P])
        ident16 = sb("ident16", [P, P], F16)
        ones = sb("ones", [P, P])
        mask = sb("mask", [P, S])
        shared = sb("shared", [P, 3 * NE * D])
        w_raw = shared[:, :].rearrange("p (m n) -> p m n", m=3)
        prob = shared[:, 0:6 * TC].rearrange("p (a i n) -> p a i n", a=2, i=3)
        oT = shared[:, 6 * TC:6 * TC + 2 * G * S].rearrange("p (a g n) -> p a g n", a=2, g=G)
        w_tern = sb("w_tern", [P, NE * D], F16)
        wT_up = sb("wT_up", [P, ND, F], F16)
        wT_gate = sb("wT_gate", [P, ND, F], F16)
        wT_down = sb("wT_down", [P, NE, D], F16)
        w_sum = sb("w_sum", [P, 3])
        w_scale = sb("w_scale", [P, 3])
        w_thr = sb("w_thr", [P, 3, 2])
        h_unit = sb("h_unit", [P, 2])
        y_scale = sb("y_scale", [P, 2])
        wq = sb("wq", [P, ND, H * DH])
        wkv = sb("wkv", [P, ND, P])
        bq_col = sb("bq_col", [P, 2])
        bkv_col = sb("bkv_col", [P, 1])
        qk_ends = sb("qk_ends", [P, 2, 4])
        qk_most = sb("qk_most", [P, 4])
        qk_bound = sb("qk_bound", [P, 4])
        qk_scale = sb("qk_scale", [P, 8])
        x = sb("x", [P, NT, D])
        stats = sb("stats", [P, TT, 6])
        mv = sb("mv", [P, TT, 2])
        var = sb("var", [P, TT])
        rstd = sb("rstd", [P, TT])
        newton = sb("newton", [P, 2, TT])
        xn = sb("xn", [P, TT, D])
        xh = sb("xh", [P, 2, ND, TC], F16)
        xl = sb("xl", [P, 2, ND, TC], F16)
        silu = sb("silu", [P, 2, TC])
        hid = sb("hid", [P, 2, TC])
        hh = sb("hh", [P, 2, NE, TC], F16)
        hl = sb("hl", [P, 2, NE, TC], F16)
        w_abs = hh[:, 1, 0:4, :].rearrange("p e n -> p (e n)")
        w_neg = hl[:, 1, 0:4, :].rearrange("p e n -> p (e n)")
        xT = sb("xT", [P, ND, TC])
        q_hi = sb("q_hi", [P, 2, TC], F16)
        q_lo = sb("q_lo", [P, 2, TC], F16)
        k_hi = sb("k_hi", [P, TC], F16)
        k_lo = sb("k_lo", [P, TC], F16)
        vT = sb("vT", [G * DH, TC])
        q_st = sb("q_st", [P, 2, H, TC], F16)
        k_st = sb("k_st", [P, 2, G, TC], F16)
        k_mx = sb("k_mx", [P, 2, G, TC], F16)
        val = sb("val", [P, 2, TT, G, VW])
        rowmax = sb("rowmax", [P, 2, QT, H])
        sm_out = sb("sm_out", [P, 2, P + S], F16)
        mx_hi = sb("mx_hi", [HH, 2, S], F16)
        mx_32 = sb("mx_32", [HH, 2, S])
        mx_lo = sb("mx_lo", [HH, 2, S], F16)
        o_rec = sb("o_rec", [P, 2, H])
        o_norm = sb("o_norm", [P, 2, D])

        bank = [ctx.enter_context(nc.psum_tensor(f"bank{i}", [P, 512], F32)) for i in range(8)]
        bank16 = [b[:, :].bitcast(F16) for b in bank]
        U, GT, ACC, TR = bank[0:2], bank[2:4], bank[4:6], bank[6:8]
        SM, ST, PV, MI = bank[0:2], bank[2:5], bank[5], bank[6:8]
        MT = PV[:, S:2 * S]

        ld_w = [sem(f"ld_w{m}") for m in range(3)]
        ld_x0, ld_x1, ld_xr = sem("ld_x0"), sem("ld_x1"), sem("ld_xr")
        ld_attn = sem("ld_attn")
        const_ready = sem("const_ready")
        pool_self = sem("pool_self")
        abs_ready = sem("abs_ready")
        wsum_ready = sem("wsum_ready")
        dve_self = sem("dve_self")
        tern_ready = sem("tern_ready")
        wtr_ready = sem("wtr_ready")
        wT_ready = sem("wT_ready")
        most_ready = sem("most_ready")
        bound_ready = sem("bound_ready")
        attn_w_ready = sem("attn_w_ready")
        ln_stats, ln_mv, ln_rstd = sem("ln_stats"), sem("ln_mv"), sem("ln_rstd")
        xn_ready = sem("xn_ready")
        xn_centred = sem("xn_centred")
        tr_ready = sem("tr_ready")
        xh_ready, xl_ready = sem("xh_ready"), sem("xl_ready")
        u_ready, g_ready = sem("u_ready"), sem("g_ready")
        silu_ready, hid_ready = sem("silu_ready"), sem("hid_ready")
        hh_ready, hl_ready = sem("hh_ready"), sem("hl_ready")
        acc_ready, res_done = sem("acc_ready"), sem("res_done")
        xT_ready = sem("xT_ready")
        qkv_ready = sem("qkv_ready")
        qkv_hi, qkv_lo = sem("qkv_hi"), sem("qkv_lo")
        vT_ready, vtr_ready, val_ready = sem("vT_ready"), sem("vtr_ready"), sem("val_ready")
        scr_written = sem("scr_written")
        st_loaded = [sem(f"st_loaded{n}") for n in range(2)]
        sm_ready, sm_done = sem("sm_ready"), sem("sm_done")
        mxT_ready, mx_ready, mxlo_ready = sem("mxT_ready"), sem("mx_ready"), sem("mxlo_ready")
        mx_loaded = [sem(f"mx_loaded{n}") for n in range(2)]
        st_ready, exp_done, prob_ready = sem("st_ready"), sem("exp_done"), sem("prob_ready")
        pv_ready, oT_ready = sem("pv_ready"), sem("oT_ready")
        otr_ready, rec_ready, onorm_ready = sem("otr_ready"), sem("rec_ready"), sem("onorm_ready")
        xadd_done = sem("xadd_done")
        out_done = sem("out_done")
        dve_passed, pe_passed, pool_passed = sem("dve_passed"), sem("pe_passed"), sem("pool_passed")

        N_SCR, N_ST = 4, 12
        NG = NB * G

        block = ctx.enter_context(nc.Block())

        @block.sync
        def _(sp):
            w_up_v = W_up.rearrange("(n p) d -> p n d", p=P)
            w_gate_v = W_gate.rearrange("(n p) d -> p n d", p=P)
            w_down_v = W_down.rearrange("(t p) e -> p t e", p=P)
            sp.dma_start(w_raw[:, 0, :].rearrange("p (n d) -> p n d", d=D), w_up_v).then_inc(ld_w[0], 16)
            sp.dma_start(x[:, 0:TT, :], x_dram[:, 0:TT, :]).then_inc(ld_x0, 16)
            sp.dma_start(w_raw[:, 1, :].rearrange("p (n d) -> p n d", d=D), w_gate_v).then_inc(ld_w[1], 16)
            sp.dma_start(w_raw[:, 2, :].rearrange("p (t e) -> p t e", e=F), w_down_v).then_inc(ld_w[2], 16)
            sp.dma_start(x[:, TT:2 * TT, :], x_dram[:, TT:2 * TT, :]).then_inc(ld_x1, 16)
            sp.dma_start(x[:, 2 * TT:NT, :], x_dram[:, 2 * TT:NT, :]).then_inc(ld_xr, 16)
            for t in range(ND):
                rows = slice(t * P, (t + 1) * P)
                sp.dma_start(wq[:, t, :].rearrange("p (h d) -> p h d", d=DH),
                             Wq[:, rows, :].rearrange("h e d -> e h d")).then_inc(ld_attn, 16)
                sp.dma_start(wkv[:, t, 0:G * DH].rearrange("p (g d) -> p g d", d=DH),
                             Wv[:, rows, :].rearrange("g e d -> e g d")).then_inc(ld_attn, 16)
                sp.dma_start(wkv[:, t, G * DH:P].rearrange("p (g d) -> p g d", d=DH),
                             Wk[:, rows, :].rearrange("g e d -> e g d")).then_inc(ld_attn, 16)
            for t in range(2):
                sp.dma_start(bq_col[:, t:t + 1],
                             bq[t * H // 2:(t + 1) * H // 2, :].rearrange("h (d a) -> (h d) a", a=1)).then_inc(ld_attn, 16)
            sp.dma_start(bkv_col[0:G * DH, :], bv.rearrange("g (d a) -> (g d) a", a=1)).then_inc(ld_attn, 16)
            sp.dma_start(bkv_col[G * DH:P, :], bk.rearrange("g (d a) -> (g d) a", a=1)).then_inc(ld_attn, 16)

            def write_scratch(c, par):
                sp.wait_ge(qkv_lo, 3 * c + 3)
                for part, k_part, q_part in ((0, k_hi, q_hi), (1, k_lo, q_lo)):
                    sp.dma_start(k_scr[par, part].rearrange("g d t -> (g d) t"),
                                 k_part[G * DH:P, :]).then_inc(scr_written, 16)
                    sp.dma_start(q_scr[par, part].rearrange("(m h) d t -> (h d) m t", m=2),
                                 q_part[:, :, :]).then_inc(scr_written, 16)

            def read_scratch(c, par):
                sp.wait_ge(scr_written, 16 * N_SCR * (c + 1))
                for n, (q_part, k_part) in enumerate(((0, 0), (1, 0), (0, 1), (1, 1))):
                    rows = slice(n * DH, (n + 1) * DH)
                    for dst, scr, part in ((k_mx, k_scr, k_part), (k_st, k_scr, k_part), (q_st, q_scr, q_part)):
                        sp.dma_start(dst[rows, par, :, :],
                                     scr[par, part].rearrange("h d t -> d h t")).then_inc(st_loaded[par], 16)

            def load_max(b, k, half):
                par, seq = k // 2 % 2, k % 2
                sp.wait_ge(mxlo_ready, 2 * b + half + 1)
                heads, cols = slice(half * HH, (half + 1) * HH), slice(seq * S, (seq + 1) * S)
                sp.dma_start(q_st[64:65, par, heads, cols], mx_hi[:, half, :]).then_inc(mx_loaded[half], 16)
                sp.dma_start(q_st[65:66, par, heads, cols], mx_lo[:, half, :]).then_inc(mx_loaded[half], 16)

            def attention_pair(pair, last):
                c0 = 2 * pair
                for k in range(4):
                    b, odd = 2 * c0 + k, k % 2
                    c, par = c0 + k // 2, k // 2
                    for g in range(G):
                        if g in (0, 2) and not (last and k == 3):
                            load_max(b + 1, k + 1, g // 2)
                        if odd and g == 1 and not last:
                            write_scratch(c + 2, par)
                        if odd and g == 2 and not last:
                            sp.wait_ge(st_ready, 3 * G * (b + 1))
                            read_scratch(c + 2, par)

            sp.wait_ge(const_ready, 3)
            write_scratch(0, 0)
            read_scratch(0, 0)
            write_scratch(1, 1)
            read_scratch(1, 1)
            load_max(0, 0, 0)
            load_max(0, 0, 1)
            with sp.Fori(0, NC // 2 - 1) as i:
                attention_pair(i, False)
            attention_pair(NC // 2 - 1, True)
            for c in range(NC):
                sp.wait_ge(res_done, 2 + NT + TT * (c + 1))
                sp.dma_start(out_dram[:, TT * c:TT * (c + 1), :],
                             x[:, TT * c:TT * (c + 1), :]).then_inc(out_done, 16)
            sp.wait_ge(out_done, 16 * NC)

        @block.gpsimd
        def _(pool):
            steps = [0]

            def step(ins):
                steps[0] += 1
                ins.then_inc(pool_self, 1)
                pool.wait_ge(pool_self, steps[0])

            step(pool.memset(ident32[:, :], 0.0))
            step(pool.affine_select(out=ident32[:, :], in_=ident32[:, :], compare_op=ALU.not_equal, fill=1.0,
                                    base=0, pattern=[[-1, P]], channel_multiplier=1))
            step(pool.tensor_copy(ident16[:, :], ident32[:, :]))
            pool.memset(ones[:, :], 1.0).then_inc(const_ready, 1)
            pool.wait_ge(const_ready, 1)
            step(pool.memset(mask[:, :], 0.0))
            step(pool.affine_select(out=mask[:, P:S], in_=mask[:, P:S], compare_op=ALU.is_ge, fill=MASKED,
                                    base=0, pattern=[[-1, P]], channel_multiplier=1))
            step(pool.memset(val[:, :, :, :, :], 0.0))
            pool.memset(val[:, :, :, :, DH:DH + 1], 1.0).then_inc(const_ready, 1)
            pool.wait_ge(const_ready, 2)
            step(pool.memset(k_st[64:P, :, :, :], 0.0))
            step(pool.memset(k_st[64:66, :, :, :], MAX_UNIT))
            step(pool.memset(k_mx[64:P, :, :, :], 0.0))
            pool.memset(q_st[64:P, :, :, :].bitcast(U32), 0).then_inc(const_ready, 1)
            pool.wait_ge(const_ready, 3)
            pool.memset(o_norm[:, :, :], 0.0).then_inc(xadd_done, 2)
            pool.wait_ge(xadd_done, 2)
            pool.wait_ge(most_ready, 1)
            pool.partition_all_reduce(qk_bound[:, :], qk_most[:, :], P, RMAX).then_inc(bound_ready, 1)

            def causal(n, par):
                pool.wait_ge(exp_done, 3 * n + 3)
                pool.sem_inc(pool_passed)
                early = prob[:, par, 0:2, :].rearrange("p i (h q) -> p (i h) q", q=S)[:, :, 0:P]
                late = prob[:, par, 2, :].rearrange("p (h q) -> p h q", q=P)
                pool.affine_select(out=early, in_=early, compare_op=ALU.is_ge, fill=0.0, base=0,
                                   pattern=[[0, HPG], [1, P]], channel_multiplier=-1)
                pool.affine_select(out=late, in_=late, compare_op=ALU.is_ge, fill=0.0, base=0,
                                   pattern=[[0, HPG], [1, P]], channel_multiplier=-1).then_inc(prob_ready, 1)

            def max_rest(b, half):
                pool.wait_ge(mx_ready, 2 * b + half + 1)
                if not isinstance(b, int) or b > 0:
                    pool.wait_ge(mx_loaded[half], 32 * b)
                pool.tensor_tensor(mx_lo[:, half, :], mx_32[:, half, :], mx_hi[:, half, :],
                                   ALU.subtract).then_inc(mxlo_ready, 1)

            def attention_pair(pair, last):
                c0 = 2 * pair
                for k in range(4):
                    b, odd = 2 * c0 + k, k % 2
                    for g in range(G):
                        end = last and k == 3
                        if g in (0, 2) and not end:
                            max_rest(b + 1, g // 2)
                        if not odd and g == 2 and not last:
                            scale_chunk(NC + c0 + k // 2 + 2)
                        if not (end and g >= 2):
                            causal(4 * b + g + 2, g % 2)
                        if not odd and g == 1 and not last:
                            centre_chunk(NC + c0 + k // 2 + 2, TT * (c0 + k // 2 + 2))
                        if odd and g == 2:
                            add_outputs(b - 1)
                    if odd:
                        add_outputs(b)

            def add_outputs(b):
                for qt in range(QT):
                    pool.wait_ge(onorm_ready, 2 * b + qt + 3)
                    tile = x[:, 2 * b + qt, :]
                    pool.tensor_tensor(tile, tile, o_norm[:, qt, :], ALU.add).then_inc(xadd_done, 1)

            def centre_chunk(q, t0):
                pool.wait_ge(ln_mv, q + 1)
                pool.wait_ge(tr_ready, 2 * q)
                pool.tensor_tensor(xn[:, :, :], x[:, bass.ds(t0, TT), :], mv[:, :, 0:1].to_broadcast([P, TT, D]),
                                   ALU.subtract).then_inc(xn_centred, 1)

            def scale_chunk(q):
                pool.wait_ge(ln_rstd, RSTD_STEPS * (q + 1))
                pool.wait_ge(xn_centred, q - NC - 1)
                pool.tensor_tensor(xn[:, :, :], xn[:, :, :], rstd[:, :].unsqueeze(2).to_broadcast([P, TT, D]),
                                   ALU.mult).then_inc(xn_ready, 1)

            max_rest(0, 0)
            max_rest(0, 1)
            causal(0, 0)
            causal(1, 1)
            with pool.Fori(0, NC // 2 - 1) as i:
                attention_pair(i, False)
            attention_pair(NC // 2 - 1, True)

        @block.scalar
        def _(act):
            def abs_sum(m):
                act.wait_ge(ld_w[m], 16)
                if m:
                    act.wait_ge(abs_ready, m)
                act.activation(w_abs, w_raw[:, m, :], ACT.Abs, accum_out=w_sum[:, m:m + 1]).then_inc(abs_ready, 1)

            def copy_weights(m):
                dst = (wT_up[:, :, :], wT_gate[:, :, :],
                       wT_down[:, :, :].rearrange("p (a n) d -> p a (n d)", a=2))[m]
                for t in range(2):
                    act.wait_ge(wtr_ready, 2 * m + t + 1)
                    act.activation(dst[:, t, :], bank16[2 * m + t], ACT.Copy).then_inc(wT_ready, 1)

            def x_high(n, q, par):
                for d in range(ND):
                    act.wait_ge(tr_ready, 2 * q + d + 1)
                    act.activation(xh[:, par, d, :], TR[d][:, :], ACT.Copy).then_inc(xh_ready, 1)

            def feed_forward(ph):
                def chunk(c, par, nxt):
                    for e in range(NE):
                        s = 64 * ph + NE * c + e
                        act.wait_ge(u_ready, s + 1)
                        if not (isinstance(s, int) and s < 2):
                            act.wait_ge(hid_ready, s - 1)
                        act.activation(silu[:, e % 2, :], U[e % 2][:, :], ACT.Silu,
                                       scale=w_scale[:, 0:1]).then_inc(silu_ready, 1)
                        act.wait_ge(hid_ready, s + 1)
                        act.activation(hh[:, par, e, :], hid[:, e % 2, :], ACT.Copy).then_inc(hh_ready, 1)
                        if nxt and e == 5:
                            x_high(NC * ph + c + 1, 2 * NC * ph + c + 1, 1 - par)
                        if ph == 0 and isinstance(c, int) and c == 0 and e == 6:
                            copy_weights(2)
                x_high(NC * ph, 2 * NC * ph, 0)
                if ph == 0:
                    copy_weights(1)
                    abs_sum(2)
                chunk(0, 0, True)
                with act.Fori(0, NC // 2 - 1) as i:
                    chunk(2 * i + 1, 1, True)
                    chunk(2 * i + 2, 0, True)
                chunk(NC - 1, 1, False)

            def xT_copy(c):
                for d in range(ND):
                    act.wait_ge(tr_ready, 2 * (NC + c) + d + 1)
                    act.activation(xT[:, d, :], MI[d][:, :], ACT.Copy).then_inc(xT_ready, 1)

            def project_high(c):
                act.wait_ge(qkv_ready, 3 * c + 1)
                act.activation(vT[:, :], MI[0][0:G * DH, :], ACT.Identity, bias=bkv_col[0:G * DH, :]).then_inc(vT_ready, 1)
                if not (isinstance(c, int) and c == 0):
                    act.wait_ge(scr_written, 16 * N_SCR * c)
                act.activation(k_hi[G * DH:P, :], MI[0][G * DH:P, :], ACT.Identity,
                               bias=bkv_col[G * DH:P, :]).then_inc(qkv_hi, 1)

            def query_high(c, m):
                act.wait_ge(qkv_ready, 3 * c + m + 2)
                act.activation(q_hi[:, m, :], MI[1 - m][:, :], ACT.Identity,
                               bias=bq_col[:, m:m + 1]).then_inc(qkv_hi, 1)

            def val_copy(c, par):
                act.wait_ge(vtr_ready, c + 1)
                act.activation(val[:, par, :, :, 0:DH],
                               MI[1][:, 0:TT * G * DH].rearrange("p (t g d) -> p t g d", t=TT, g=G),
                               ACT.Copy).then_inc(val_ready, 1)

            def max_copy(b, half):
                act.wait_ge(mxT_ready, 2 * b + half + 1)
                if not (isinstance(b, int) and b == 0):
                    act.wait_ge(mx_loaded[half], 32 * b)
                act.activation(mx_hi[:, half, :], MT[0:HH, :], ACT.Copy, scale=-1.0 / MAX_UNIT)
                act.activation(mx_32[:, half, :], MT[0:HH, :], ACT.Copy,
                               scale=-1.0 / MAX_UNIT).then_inc(mx_ready, 1)

            def exps(n, par):
                for i in range(3):
                    act.wait_ge(st_ready, 3 * n + i + 1)
                    act.activation(prob[:, par, i, :], ST[i][:, :], ACT.Exp,
                                   scale=qk_scale[:, 4:5]).then_inc(exp_done, 1)

            def attention_pair(pair, last):
                c0 = 2 * pair
                for k in range(4):
                    b, odd = 2 * c0 + k, k % 2
                    c, par = c0 + k // 2, k // 2
                    for g in range(G):
                        n, end = 4 * b + g, last and k == 3
                        act.wait_ge(pv_ready, n + 1)
                        if g in (0, 2) and not end:
                            max_copy(b + 1, g // 2)
                        act.activation(oT[:, odd, g, :], PV[:, 0:S], ACT.Copy).then_inc(oT_ready, 1)
                        if not (end and g >= 2):
                            exps(n + 2, g % 2)
                        if not last:
                            if not odd and g == 3:
                                xT_copy(c + 2)
                            if odd and g == 0:
                                project_high(c + 2)
                                query_high(c + 2, 0)
                            if odd and g == 1:
                                query_high(c + 2, 1)
                            if odd and g == 3:
                                val_copy(c + 2, par)

            def attention():
                act.wait_ge(attn_w_ready, 3)
                for c in range(2):
                    xT_copy(c)
                    project_high(c)
                    query_high(c, 0)
                    query_high(c, 1)
                    val_copy(c, c)
                max_copy(0, 0)
                max_copy(0, 1)
                act.sem_inc(oT_ready)
                exps(0, 0)
                exps(1, 1)
                with act.Fori(0, NC // 2 - 1) as i:
                    attention_pair(i, False)
                attention_pair(NC // 2 - 1, True)

            abs_sum(0)
            abs_sum(1)
            copy_weights(0)
            feed_forward(0)
            attention()
            feed_forward(1)

        @block.vector
        def _(dve):
            steps = [0]

            def step(ins):
                steps[0] += 1
                ins.then_inc(dve_self, 1)
                dve.wait_ge(dve_self, steps[0])

            def scale_of(m):
                dve.wait_ge(wsum_ready, m + 1)
                step(dve.tensor_scalar(w_scale[:, m:m + 1], ACC[m % 2][:, 0:1], 1.0 / (F * D), QUANT_EPS,
                                       ALU.mult, ALU.add))
                dve.tensor_scalar(w_thr[:, m, 0:1], w_scale[:, m:m + 1], 0.5, None, ALU.mult)
                step(dve.tensor_scalar(w_thr[:, m, 1:2], w_scale[:, m:m + 1], -0.5, None, ALU.mult))

            def ternary(m):
                if m:
                    dve.wait_ge(wtr_ready, 2 * m)
                step(dve.tensor_scalar(w_neg, w_raw[:, m, :], w_thr[:, m, 1:2], None, ALU.is_lt))
                dve.scalar_tensor_tensor(out=w_tern[:, :], in0=w_raw[:, m, :], scalar=w_thr[:, m, 0:1],
                                         in1=w_neg, op0=ALU.is_gt, op1=ALU.subtract).then_inc(tern_ready, 1)

            def ln_1(q, t0):
                for t in range(TT):
                    ins = dve.bn_stats(stats[:, t, :], x[:, t0 + t, :])
                ins.then_inc(ln_stats, 1)

            def ln_2(q):
                dve.wait_ge(ln_stats, q + 1)
                if not (isinstance(q, int) and q == 0):
                    dve.wait_ge(xn_ready, q)
                dve.sem_inc(dve_passed)
                for t in range(TT):
                    ins = dve.bn_aggr(mv[:, t, :], stats[:, t, :])
                ins.then_inc(ln_mv, 1)

            def ln_3(q):
                dve.wait_ge(ln_mv, q + 1)
                dve.tensor_scalar(var[:, :], mv[:, :, 1], LN_EPS, None, ALU.add).then_inc(ln_rstd, 1)
                dve.wait_ge(ln_rstd, RSTD_STEPS * q + 1)
                dve.tensor_scalar(rstd[:, :].bitcast(U32), var[:, :].bitcast(U32), 1, None,
                                  ALU.logical_shift_right).then_inc(ln_rstd, 1)
                dve.wait_ge(ln_rstd, RSTD_STEPS * q + 2)
                dve.tensor_scalar(rstd[:, :].bitcast(I32), rstd[:, :].bitcast(I32), -1.0, float(RSQRT_GUESS),
                                  ALU.mult, ALU.add).then_inc(ln_rstd, 1)
                for n in range(3):
                    dve.wait_ge(ln_rstd, RSTD_STEPS * q + 3 + 3 * n)
                    dve.tensor_tensor(newton[:, 0, :], var[:, :], rstd[:, :], ALU.mult).then_inc(ln_rstd, 1)
                    dve.wait_ge(ln_rstd, RSTD_STEPS * q + 4 + 3 * n)
                    dve.scalar_tensor_tensor(out=newton[:, 1, :], in0=newton[:, 0, :], scalar=-0.5, in1=rstd[:, :],
                                             op0=ALU.mult, op1=ALU.mult).then_inc(ln_rstd, 1)
                    dve.wait_ge(ln_rstd, RSTD_STEPS * q + 5 + 3 * n)
                    dve.scalar_tensor_tensor(out=rstd[:, :], in0=newton[:, 1, :], scalar=1.5, in1=rstd[:, :],
                                             op0=ALU.add, op1=ALU.mult).then_inc(ln_rstd, 1)

            def ln_4(q, t0):
                dve.wait_ge(ln_rstd, RSTD_STEPS * (q + 1))
                if not (isinstance(q, int) and q == 0):
                    dve.wait_ge(tr_ready, 2 * q)
                for t in range(TT):
                    ins = dve.tensor_scalar(xn[:, t, :], x[:, t0 + t, :], mv[:, t, 0:1], rstd[:, t:t + 1],
                                            ALU.subtract, ALU.mult)
                ins.then_inc(xn_ready, 1)

            def x_low(n, par):
                for d in range(ND):
                    dve.wait_ge(xh_ready, 2 * n + d + 1)
                    dve.tensor_tensor(xl[:, par, d, :], TR[d][:, :], xh[:, par, d, :],
                                      ALU.subtract).then_inc(xl_ready, 1)

            def feed_forward(ph):
                def chunk(c, par, down, nxt):
                    q = 2 * NC * ph + c + 1
                    first = isinstance(c, int) and c == 0
                    for e in range(NE):
                        s = 64 * ph + NE * c + e
                        if nxt and e == 0:
                            if ph:
                                dve.wait_ge(xadd_done, 2 + TT * (c + 2))
                            else:
                                dve.wait_ge(ld_x1 if first else ld_xr, 16)
                            ln_1(q, TT * (c + 1))
                        dve.wait_ge(silu_ready, s + 1)
                        dve.wait_ge(g_ready, s + 1)
                        dve.scalar_tensor_tensor(out=hid[:, e % 2, :], in0=silu[:, e % 2, :], scalar=h_unit[:, 0:1],
                                                 in1=GT[e % 2][:, :], op0=ALU.mult, op1=ALU.mult).then_inc(hid_ready, 1)
                        if nxt and e == 1:
                            ln_2(q)
                        if nxt and e == 2:
                            ln_3(q)
                        if nxt and e == 3:
                            ln_4(q, TT * (c + 1))
                        if ph == 0 and first and e == 1:
                            scale_of(2)
                            ternary(2)
                            step(dve.tensor_tensor(y_scale[:, 0:1], w_scale[:, 0:1], w_scale[:, 1:2], ALU.mult))
                            step(dve.tensor_tensor(y_scale[:, 1:2], y_scale[:, 0:1], w_scale[:, 2:3], ALU.mult))
                        dve.wait_ge(hh_ready, s + 1)
                        dve.tensor_tensor(hl[:, par, e, :], hid[:, e % 2, :], hh[:, par, e, :],
                                          ALU.subtract).then_inc(hl_ready, 1)
                        if nxt and e == 5:
                            x_low(NC * ph + c + 1, 1 - par)
                        if down and e % 2:
                            residual(c - 1, e // 2)

                def residual(c, t):
                    dve.wait_ge(acc_ready, NT * ph + TT * c + t + 1)
                    tile = x[:, TT * c + t, :]
                    dve.scalar_tensor_tensor(out=tile, in0=ACC[t % 2][:, 0:D], scalar=y_scale[:, 1:2], in1=tile,
                                             op0=ALU.mult, op1=ALU.add).then_inc(res_done, 1)

                q0 = 2 * NC * ph
                if ph:
                    dve.wait_ge(xadd_done, 2 + TT)
                else:
                    dve.wait_ge(ld_x0, 16)
                ln_1(q0, 0)
                ln_2(q0)
                ln_3(q0)
                ln_4(q0, 0)
                if ph == 0:
                    scale_of(1)
                    ternary(1)
                x_low(NC * ph, 0)
                chunk(0, 0, False, True)
                with dve.Fori(0, NC // 2 - 1) as i:
                    chunk(2 * i + 1, 1, True, True)
                    chunk(2 * i + 2, 0, True, True)
                chunk(NC - 1, 1, True, False)
                for t in range(TT):
                    residual(NC - 1, t)

            def scale_projections():
                dve.wait_ge(ld_attn, 16 * 10)
                step(dve.memset(qk_ends[:, :, :], 0.0))
                for n, op in enumerate((ALU.max, ALU.min)):
                    dve.tensor_reduce(qk_ends[:, n, 0:1], wq[:, :, :].rearrange("p t n -> p (t n)"), AXX, op)
                    dve.tensor_reduce(qk_ends[:, n, 1:2], wkv[:, :, G * DH:P], mybir.AxisListType.XY, op)
                    dve.tensor_reduce(qk_ends[:, n, 2:3], bq_col[:, :], AXX, op)
                    ins = dve.tensor_copy(qk_ends[G * DH:P, n, 3:4], bkv_col[G * DH:P, :])
                step(ins)
                dve.scalar_tensor_tensor(out=qk_most[:, :], in0=qk_ends[:, 1, :], scalar=-1.0, in1=qk_ends[:, 0, :],
                                         op0=ALU.mult, op1=ALU.max).then_inc(most_ready, 1)
                dve.wait_ge(bound_ready, 1)
                step(dve.scalar_tensor_tensor(out=qk_scale[:, 0:2], in0=qk_bound[:, 0:2], scalar=float(D),
                                              in1=qk_bound[:, 2:4], op0=ALU.mult, op1=ALU.add))
                step(dve.tensor_scalar(qk_scale[:, 0:2], qk_scale[:, 0:2], 1e-12, None, ALU.max))
                step(dve.reciprocal(qk_scale[:, 2:4], qk_scale[:, 0:2]))
                step(dve.tensor_scalar(qk_scale[:, 2:4].bitcast(U32), qk_scale[:, 2:4].bitcast(U32), EXPONENT_BITS, None,
                                       ALU.bitwise_and))
                step(dve.tensor_scalar(qk_scale[:, 2:4], qk_scale[:, 2:4], QK_BOUND, None, ALU.mult))
                step(dve.tensor_tensor(qk_scale[:, 5:6], qk_scale[:, 2:3], qk_scale[:, 3:4], ALU.mult))
                step(dve.reciprocal(qk_scale[:, 6:7], qk_scale[:, 5:6]))
                dve.tensor_scalar(qk_scale[:, 4:5], qk_scale[:, 6:7], float(DH) ** -0.5, None,
                                  ALU.mult).then_inc(attn_w_ready, 1)
                all_q = wq[:, :, :].rearrange("p t n -> p (t n)")
                dve.tensor_scalar(all_q, all_q, qk_scale[:, 2:3], None, ALU.mult)
                dve.tensor_scalar(wkv[:, :, G * DH:P], wkv[:, :, G * DH:P], qk_scale[:, 3:4], None,
                                  ALU.mult).then_inc(attn_w_ready, 1)
                dve.tensor_scalar(bq_col[:, :], bq_col[:, :], qk_scale[:, 2:3], None, ALU.mult)
                dve.tensor_scalar(bkv_col[G * DH:P, :], bkv_col[G * DH:P, :], qk_scale[G * DH:P, 3:4], None,
                                  ALU.mult).then_inc(attn_w_ready, 1)

            def key_low(c):
                dve.wait_ge(qkv_hi, 3 * c + 1)
                dve.scalar_tensor_tensor(out=k_lo[G * DH:P, :], in0=MI[0][G * DH:P, :], scalar=bkv_col[G * DH:P, :],
                                         in1=k_hi[G * DH:P, :], op0=ALU.add, op1=ALU.subtract).then_inc(qkv_lo, 1)

            def query_low(c, m):
                dve.wait_ge(qkv_hi, 3 * c + m + 2)
                dve.scalar_tensor_tensor(out=q_lo[:, m, :], in0=MI[1 - m][:, :], scalar=bq_col[:, m:m + 1],
                                         in1=q_hi[:, m, :], op0=ALU.add, op1=ALU.subtract).then_inc(qkv_lo, 1)

            def row_max(n, seq_par, g, heads=range(HPG)):
                for j in heads:
                    h = HPG * g + j
                    dve.wait_ge(sm_ready, HPG * n + j + 1)
                    dve.sem_inc(dve_passed)
                    dve.tensor_tensor_reduce(sm_out[:, j % 2, 0:P], SM[j % 2][:, 0:P], mask[:, P:S], 1.0, MASKED,
                                             ALU.add, ALU.max, rowmax[:, seq_par, 0, h:h + 1])
                    dve.tensor_tensor_reduce(sm_out[:, j % 2, P:P + S], SM[j % 2][:, P:P + S], mask[:, :], 1.0, MASKED,
                                             ALU.add, ALU.max, rowmax[:, seq_par, 1, h:h + 1]).then_inc(sm_done, 1)

            def normalise(b):
                heads = [MI[qt][:, :].rearrange("p (h w) -> p h w", w=VW) for qt in range(QT)]
                for qt in range(QT):
                    dve.wait_ge(otr_ready, 2 * b + qt + 1)
                    dve.reciprocal(o_rec[:, qt, :], heads[qt][:, :, DH]).then_inc(rec_ready, 1)
                for qt in range(QT):
                    dve.wait_ge(rec_ready, 2 * b + qt + 1)
                    dve.wait_ge(xadd_done, 2 * b + qt + 1)
                    dve.tensor_tensor(o_norm[:, qt, :].rearrange("p (h d) -> p h d", d=DH), heads[qt][:, :, 0:DH],
                                      o_rec[:, qt, :].unsqueeze(2).to_broadcast([P, H, DH]),
                                      ALU.mult).then_inc(onorm_ready, 1)

            def attention_pair(pair, last):
                c0 = 2 * pair
                for k in range(4):
                    b, odd = 2 * c0 + k, k % 2
                    c = c0 + k // 2
                    q = NC + c + 2
                    for g in range(G):
                        lead = (4 * b + g + 6, (k + (g + 6) // 4) % 2, (g + 2) % 4)
                        ahead = not (last and (k == 3 or (k == 2 and g >= 2)))
                        if ahead:
                            row_max(*lead, range(0, 2))
                        if not odd and not last:
                            if g == 0:
                                ln_1(q, TT * (c + 2))
                                ln_2(q)
                            if g == 1:
                                ln_3(q)
                        if odd and not last:
                            if g == 0:
                                key_low(c + 2)
                                query_low(c + 2, 0)
                            if g == 1:
                                query_low(c + 2, 1)
                        if odd and g == 2:
                            normalise(b - 1)
                        if ahead:
                            row_max(*lead, range(2, HPG))
                        if odd and g == 3:
                            normalise(b)

            def attention():
                for c in range(2):
                    q = NC + c
                    dve.wait_ge(res_done, 2 + TT * (c + 1))
                    ln_1(q, TT * c)
                    ln_2(q)
                    ln_3(q)
                    ln_4(q, TT * c)
                    key_low(c)
                    query_low(c, 0)
                    query_low(c, 1)
                dve.wait_ge(const_ready, 2)
                for n in range(6):
                    row_max(n, n // G, n % G)
                dve.wait_ge(val_ready, 2)
                dve.memset(o_rec[:, 0, 0:1], 0.0).then_inc(onorm_ready, 2)
                with dve.Fori(0, NC // 2 - 1) as i:
                    attention_pair(i, False)
                attention_pair(NC // 2 - 1, True)

            scale_of(0)
            step(dve.reciprocal(h_unit[:, 1:2], w_scale[:, 0:1]))
            step(dve.tensor_scalar(h_unit[:, 0:1], h_unit[:, 1:2], 0.5, None, ALU.mult))
            ternary(0)
            dve.memset(newton[:, :, :], 0.0).then_inc(res_done, 2)
            feed_forward(0)
            scale_projections()
            attention()
            feed_forward(1)

        @block.tensor
        def _(pe):
            def weight_sum(m):
                pe.wait_ge(abs_ready, m + 1)
                if m == 2:
                    pe.wait_ge(tern_ready, 1)
                pe.matmul(ACC[m % 2][:, 0:1], ones[:, :], w_sum[:, m:m + 1], start=True, stop=True).then_inc(wsum_ready, 1)

            def weight_transposes(m):
                pe.wait_ge(tern_ready, m + 1)
                for t in range(2):
                    for j in range(8):
                        n, d = (j, t) if m < 2 else (4 * t + j // 2, j % 2)
                        at = n * D + d * P if m < 2 else d * F + n * P
                        ins = pe.transpose(bank16[2 * m + t][:, j * P:(j + 1) * P], w_tern[:, at:at + P], ident16[:, :])
                    ins.then_inc(wtr_ready, 1)

            def x_transposes(q, ready):
                pe.wait_ge(xn_ready, q + 1)
                for d in range(ND):
                    for ready_sem, count in ready[d]:
                        pe.wait_ge(ready_sem, count)
                    for t in range(TT):
                        ins = pe.transpose(TR[d][:, t * P:(t + 1) * P], xn[:, t, d * P:(d + 1) * P], ident32[:, :])
                    ins.then_inc(tr_ready, 1)

            def feed_forward(ph):
                def up_gate(s, e, par):
                    for w, banks, done in ((wT_up, U, u_ready), (wT_gate, GT, g_ready)):
                        if not (isinstance(s, int) and s < 2):
                            pe.wait_ge(silu_ready if w is wT_up else hid_ready, s - 1)
                        for d in range(ND):
                            for part in (xh, xl):
                                ins = pe.matmul(banks[e % 2][:, :], w[:, d, e * P:(e + 1) * P], part[:, par, d, :],
                                                start=(d == 0 and part is xh), stop=(d == ND - 1 and part is xl))
                        ins.then_inc(done, 1)

                def down_half(c, par, t, half):
                    n = NT * ph + TT * c + t
                    if half == 0:
                        pe.wait_ge(res_done, n + 1)
                    for e in range(half * 4, half * 4 + 4):
                        for part in (hh, hl):
                            ins = pe.matmul(ACC[t % 2][:, 0:D], part[:, par, e, t * P:(t + 1) * P], wT_down[:, e, :],
                                            start=(e == 0 and part is hh), stop=(e == NE - 1 and part is hl))
                    if half:
                        ins.then_inc(acc_ready, 1)

                def chunk(c, par, down, nxt):
                    n = NC * ph + c
                    pe.wait_ge(xl_ready, 2 * n + 2)
                    for e in range(NE):
                        s = 64 * ph + NE * c + e
                        up_gate(s, e, par)
                        if down:
                            if e == 0:
                                pe.wait_ge(hl_ready, s)
                            down_half(c - 1, 1 - par, e // 2, e % 2)
                        if nxt and e == 4:
                            x_transposes(2 * NC * ph + c + 1, [[(xl_ready, 2 * n + 1)], [(xl_ready, 2 * n + 2)]])
                        if ph == 0 and isinstance(c, int) and c == 0:
                            if e == 0:
                                weight_sum(2)
                            if e == 5:
                                weight_transposes(2)

                if ph == 0:
                    x_transposes(0, [[], []])
                    weight_transposes(1)
                    pe.wait_ge(wT_ready, 4)
                else:
                    x_transposes(2 * NC, [[(onorm_ready, 2 * NB + 1)], [(onorm_ready, 2 * NB + 2)]])
                chunk(0, 0, False, True)
                if ph == 0:
                    pe.wait_ge(wT_ready, 6)
                with pe.Fori(0, NC // 2 - 1) as i:
                    chunk(2 * i + 1, 1, True, True)
                    chunk(2 * i + 2, 0, True, True)
                chunk(NC - 1, 1, True, False)
                pe.wait_ge(hl_ready, 64 * (ph + 1))
                for t in range(TT):
                    down_half(NC - 1, 1, t, 0)
                    down_half(NC - 1, 1, t, 1)

            def project(c, m):
                w = wkv[:, :, :] if m == 0 else wq[:, :, (m - 1) * P:m * P]
                for d in range(ND):
                    ins = pe.matmul(MI[m % 2][:, :], w[:, d, :], xT[:, d, :], start=(d == 0), stop=(d == ND - 1))
                ins.then_inc(qkv_ready, 1)

            def project_first(c):
                pe.wait_ge(xT_ready, 2 * c + 2)
                project(c, 0)
                project(c, 1)

            def project_last(c):
                pe.wait_ge(qkv_lo, 3 * c + 1)
                project(c, 2)

            def val_transposes(c, last_reader):
                pe.wait_ge(vT_ready, c + 1)
                pe.wait_ge(*last_reader)
                pe.sem_inc(pe_passed)
                for t in range(TT):
                    ins = pe.transpose(MI[1][:, t * G * DH:(t + 1) * G * DH], vT[:, t * P:(t + 1) * P],
                                       ident32[0:G * DH, 0:G * DH])
                ins.then_inc(vtr_ready, 1)

            def max_scores(n, k, g, heads=range(HPG)):
                par, seq = k // 2 % 2, k % 2
                for j in heads:
                    h = HPG * g + j
                    if not (isinstance(n, int) and n == 0 and j < 2):
                        pe.wait_ge(sm_done, HPG * n + j - 1)
                    for qt in range(QT):
                        at = seq * S
                        ins = pe.matmul(SM[j % 2][:, qt * P:qt * P + (qt + 1) * P],
                                        q_st[:, par, h, at + qt * P:at + (qt + 1) * P],
                                        k_mx[:, par, g, at:at + (qt + 1) * P], start=True, stop=True)
                    ins.then_inc(sm_ready, 1)

            def max_transposes(b, k, half):
                pe.wait_ge(sm_done, H * b + HH * (half + 1))
                if not (isinstance(b, int) and b == 0 and half == 0):
                    pe.wait_ge(mx_ready, 2 * b + half)
                for qt in range(QT):
                    ins = pe.transpose(MT[0:HH, qt * P:(qt + 1) * P], rowmax[:, k % 2, qt, half * HH:(half + 1) * HH],
                                       ident32[:, :])
                ins.then_inc(mxT_ready, 1)

            def scores(n, b, k, g):
                par, seq = k // 2 % 2, k % 2
                if g % 2 == 0:
                    pe.wait_ge(mx_loaded[g // 2], 32 * (b + 1))
                at, heads = seq * S, slice(HPG * g, HPG * (g + 1))
                for i in range(3):
                    if not (isinstance(n, int) and n == 0):
                        pe.wait_ge(exp_done, 3 * n + i - 2)
                    if i < 2:
                        keys, queries = at, q_st[:, par, HPG * g + 2 * i:HPG * g + 2 * i + 2, at:at + S]
                    else:
                        keys, queries = at + P, q_st[:, par, heads, at + P:at + S]
                    pe.matmul(ST[i][:, :], k_st[:, par, g, keys:keys + P], queries,
                              start=True, stop=True).then_inc(st_ready, 1)

            def outputs(n, k, g):
                par, seq = k // 2 % 2, k % 2
                pe.wait_ge(prob_ready, n + 1)
                for j in range(HPG):
                    rows = slice(VW * j, VW * (j + 1))
                    pe.matmul(PV[rows, 0:S], val[:, par, QT * seq, g, :],
                              prob[:, g % 2, j // 2, (j % 2) * S:(j % 2 + 1) * S], start=True, stop=False,
                              tile_position=(0, VW * j))
                for j in range(HPG):
                    rows = slice(VW * j, VW * (j + 1))
                    ins = pe.matmul(PV[rows, P:S], val[:, par, QT * seq + 1, g, :],
                                    prob[:, g % 2, 2, j * P:(j + 1) * P], start=False, stop=True,
                                    tile_position=(0, VW * j))
                ins.then_inc(pv_ready, 1)

            def output_transposes(b, k, prev):
                pe.wait_ge(oT_ready, G * (b + 1) + 1)
                for qt in range(QT):
                    pe.wait_ge(*prev[qt])
                    for g in range(G):
                        ins = pe.transpose(MI[qt][:, g * P:(g + 1) * P], oT[:, k % 2, g, qt * P:(qt + 1) * P], ident32[:, :])
                    ins.then_inc(otr_ready, 1)

            def attention_pair(pair, last):
                c0 = 2 * pair
                for k in range(4):
                    b, odd = 2 * c0 + k, k % 2
                    c, par = c0 + k // 2, k // 2
                    for g in range(G):
                        n, end = 4 * b + g, last and k == 3
                        lead = (n + 6, k + (g + 6) // 4, (g + 2) % 4)
                        ahead = not (end or (last and k == 2 and g >= 2))
                        if ahead:
                            if not odd and g == 2:
                                pe.wait_ge(st_loaded[1 - par], 16 * N_ST * (pair + par + 1))
                            max_scores(*lead, range(0, 1))
                        if g == 0 and not odd:
                            pe.wait_ge(val_ready, c + 1)
                        pe.wait_ge(oT_ready, n + 1)
                        if g in (0, 2) and not end:
                            max_transposes(b + 1, k + 1, g // 2)
                        outputs(n, k, g)
                        if ahead:
                            max_scores(*lead, range(1, 2))
                        if not (end and g >= 2):
                            scores(n + 2, b + (g + 2) // 4, k + (g + 2) // 4, (g + 2) % 4)
                        if not last:
                            if not odd and g == 3:
                                x_transposes(NC + c + 2, [[(onorm_ready, 2 * b + 1)], [(onorm_ready, 2 * b + 2)]])
                            if odd and g == 0:
                                project_first(c + 2)
                            if odd and g == 1:
                                project_last(c + 2)
                            if odd and g == 3:
                                val_transposes(c + 2, (onorm_ready, 2 * b + 2))
                        if ahead:
                            max_scores(*lead, range(2, 3))
                        if odd and g == 2:
                            output_transposes(b - 1, k - 1, [(onorm_ready, 2 * b - 1), (onorm_ready, 2 * b)] if last
                                              else [(qkv_lo, 3 * (c + 2) + 3)] * 2)
                        if ahead:
                            max_scores(*lead, range(3, HPG))
                        if odd and g == 3:
                            output_transposes(b, k, [(onorm_ready, 2 * b + 1),
                                                     (onorm_ready, 2 * b + 2) if last else (val_ready, c + 3)])

            def attention():
                pe.wait_ge(attn_w_ready, 3)
                pe.wait_ge(res_done, NT + 2)
                for c in range(2):
                    x_transposes(NC + c, [[(xl_ready, 2 * NC)], [(xl_ready, 2 * NC)]] if c == 0
                                 else [[(qkv_lo, 3)], [(val_ready, 1)]])
                    project_first(c)
                    project_last(c)
                    val_transposes(c, (qkv_lo, 3 * c + 2))
                pe.wait_ge(st_loaded[0], 16 * N_ST)
                for n in range(6):
                    max_scores(n, n // G, n % G)
                    if n in (2, 4):
                        max_transposes(0, 0, n // 2 - 1)
                pe.wait_ge(val_ready, 2)
                for n in range(2):
                    scores(n, 0, 0, n)
                with pe.Fori(0, NC // 2 - 1) as i:
                    attention_pair(i, False)
                attention_pair(NC // 2 - 1, True)

            pe.wait_ge(const_ready, 1)
            weight_sum(0)
            weight_sum(1)
            weight_transposes(0)
            feed_forward(0)
            attention()
            feed_forward(1)


_INS = ["L0_attn_x", "L0_attn_Wq", "L0_attn_bq", "L0_attn_Wk", "L0_attn_bk", "L0_attn_Wv", "L0_attn_bv",
        "L0_ffn_W_up", "L0_ffn_W_gate", "L0_ffn_W_down"]
_OUT = ((16, 256, 256), "float32")


def kernel(**inputs):
    import numpy as _np
    import concourse.bacc as _bacc
    from concourse import mybir as _mybir
    from concourse.bass_utils import run_bass_kernel_spmd as _run

    nc = _bacc.Bacc("TRN2", target_bir_lowering=False, num_devices=1)
    arrays, args = {}, []
    for name in _INS:
        a = _np.ascontiguousarray(inputs[name])
        arrays[f"in_{name}_dram"] = a
        args.append(nc.dram_tensor(f"in_{name}_dram", a.shape, _mybir.dt.from_np(a.dtype), kind="ExternalInput").ap())
    shape, dtype = _OUT
    out = nc.dram_tensor("out_0_dram", shape, _mybir.dt.from_np(_np.dtype(dtype)), kind="ExternalOutput").ap()
    macaron_block(nc, *args, out)
    r = _run(nc, [arrays], core_ids=[0])
    return r.results[0]["out_0_dram"]
```

```python
from contextlib import ExitStack

import concourse.bass as bass
from concourse import mybir

P = 128
ALU = mybir.AluOpType
ACT = mybir.ActivationFunctionType
AXX = mybir.AxisListType.X
F32 = mybir.dt.float32
F16 = mybir.dt.float16
U32 = mybir.dt.uint32
I32 = mybir.dt.int32
RMAX = bass.bass_isa.ReduceOp.max

LN_EPS = 1e-5
QUANT_EPS = 1e-8
MASKED = -1e30
QK_BOUND = 2048.0
MAX_UNIT = 4096.0
EXPONENT_BITS = 0x7F800000
RSQRT_GUESS = 0x5F3759DF
RSTD_STEPS = 12


def macaron_block(nc, x_in, Wq, bq, Wk, bk, Wv, bv, W_up, W_gate, W_down, out):
    NB, S, D = x_in.shape
    H, _, DH = Wq.shape
    G = Wk.shape[0]
    HPG = H // G
    F = W_up.shape[0]
    ND = D // P
    NE = F // P
    TC = 512
    TT = TC // P
    NC = NB * S // TC
    BC = TC // S
    QT = S // P
    NT = NC * TT
    HH = H // 2
    VW = 32
    assert (ND, NE, TT, BC, QT, HPG, DH) == (2, 8, 4, 2, 2, 4, 16)

    x_dram = x_in.rearrange("b (t p) d -> p (b t) d", p=P)
    out_dram = out.rearrange("b (t p) d -> p (b t) d", p=P)
    q_scr = nc.dram_tensor("q_scratch", (2, 2, H, DH, TC), F16)
    k_scr = nc.dram_tensor("k_scratch", (2, 2, G, DH, TC), F16)

    with ExitStack() as ctx:
        def sb(name, shape, dt=F32):
            return ctx.enter_context(nc.sbuf_tensor(name, shape, dt))

        def sem(name):
            return ctx.enter_context(nc.semaphore(name))

        ident32 = sb("ident32", [P, P])
        ident16 = sb("ident16", [P, P], F16)
        ones = sb("ones", [P, P])
        mask = sb("mask", [P, S])
        shared = sb("shared", [P, 3 * NE * D])
        w_raw = shared[:, :].rearrange("p (m n) -> p m n", m=3)
        prob = shared[:, 0:6 * TC].rearrange("p (a i n) -> p a i n", a=2, i=3)
        oT = shared[:, 6 * TC:6 * TC + 2 * G * S].rearrange("p (a g n) -> p a g n", a=2, g=G)
        w_tern = sb("w_tern", [P, NE * D], F16)
        wT_up = sb("wT_up", [P, ND, F], F16)
        wT_gate = sb("wT_gate", [P, ND, F], F16)
        wT_down = sb("wT_down", [P, NE, D], F16)
        w_sum = sb("w_sum", [P, 3])
        w_scale = sb("w_scale", [P, 3])
        w_thr = sb("w_thr", [P, 3, 2])
        h_unit = sb("h_unit", [P, 2])
        y_scale = sb("y_scale", [P, 2])
        wq = sb("wq", [P, ND, H * DH])
        wkv = sb("wkv", [P, ND, P])
        bq_col = sb("bq_col", [P, 2])
        bkv_col = sb("bkv_col", [P, 1])
        qk_ends = sb("qk_ends", [P, 2, 4])
        qk_most = sb("qk_most", [P, 4])
        qk_bound = sb("qk_bound", [P, 4])
        qk_scale = sb("qk_scale", [P, 8])
        x = sb("x", [P, NT, D])
        stats = sb("stats", [P, TT, 6])
        mv = sb("mv", [P, TT, 2])
        var = sb("var", [P, TT])
        rstd = sb("rstd", [P, TT])
        newton = sb("newton", [P, 2, TT])
        xn = sb("xn", [P, TT, D])
        xh = sb("xh", [P, 2, ND, TC], F16)
        xl = sb("xl", [P, 2, ND, TC], F16)
        silu = sb("silu", [P, 2, TC])
        hid = sb("hid", [P, 2, TC])
        hh = sb("hh", [P, 2, NE, TC], F16)
        hl = sb("hl", [P, 2, NE, TC], F16)
        w_abs = hh[:, 1, 0:4, :].rearrange("p e n -> p (e n)")
        w_neg = hl[:, 1, 0:4, :].rearrange("p e n -> p (e n)")
        xT = sb("xT", [P, ND, TC])
        q_hi = sb("q_hi", [P, 2, TC], F16)
        q_lo = sb("q_lo", [P, 2, TC], F16)
        k_hi = sb("k_hi", [P, TC], F16)
        k_lo = sb("k_lo", [P, TC], F16)
        vT = sb("vT", [G * DH, TC])
        q_st = sb("q_st", [P, 2, H, TC], F16)
        k_st = sb("k_st", [P, 2, G, TC], F16)
        k_mx = sb("k_mx", [P, 2, G, TC], F16)
        val = sb("val", [P, 2, TT, G, VW])
        rowmax = sb("rowmax", [P, 2, QT, H])
        sm_out = sb("sm_out", [P, 3, 2 * S], F16)
        mx_hi = sb("mx_hi", [HH, 2, S], F16)
        mx_32 = sb("mx_32", [HH, 2, S])
        mx_lo = sb("mx_lo", [HH, 2, S], F16)
        o_rec = sb("o_rec", [P, 2, H])
        o_norm = sb("o_norm", [P, 2, D])

        bank = [ctx.enter_context(nc.psum_tensor(f"bank{i}", [P, 512], F32)) for i in range(8)]
        bank16 = [b[:, :].bitcast(F16) for b in bank]
        U, GT, ACC, TR = bank[0:2], bank[2:4], bank[4:6], bank[6:8]
        SM, ST, PV, MI = bank[0:3], bank[3:5], bank[5], bank[6:8]
        MT = PV[:, S:2 * S]

        ld_w = [sem(f"ld_w{m}") for m in range(3)]
        ld_x0, ld_x1, ld_xr = sem("ld_x0"), sem("ld_x1"), sem("ld_xr")
        ld_attn = sem("ld_attn")
        const_ready = sem("const_ready")
        pool_self = sem("pool_self")
        abs_ready = sem("abs_ready")
        wsum_ready = sem("wsum_ready")
        dve_self = sem("dve_self")
        tern_ready = sem("tern_ready")
        wtr_ready = sem("wtr_ready")
        wT_ready = sem("wT_ready")
        most_ready = sem("most_ready")
        bound_ready = sem("bound_ready")
        attn_w_ready = sem("attn_w_ready")
        ln_stats, ln_mv, ln_rstd = sem("ln_stats"), sem("ln_mv"), sem("ln_rstd")
        xn_ready = sem("xn_ready")
        xn_centred = sem("xn_centred")
        tr_ready = sem("tr_ready")
        xh_ready, xl_ready = sem("xh_ready"), sem("xl_ready")
        u_ready, g_ready = sem("u_ready"), sem("g_ready")
        silu_ready, hid_ready = sem("silu_ready"), sem("hid_ready")
        hh_ready, hl_ready = sem("hh_ready"), sem("hl_ready")
        acc_ready, res_done = sem("acc_ready"), sem("res_done")
        xT_ready = sem("xT_ready")
        qkv_ready = sem("qkv_ready")
        qkv_hi, qkv_lo = sem("qkv_hi"), sem("qkv_lo")
        vT_ready, vtr_ready, val_ready = sem("vT_ready"), sem("vtr_ready"), sem("val_ready")
        scr_written = sem("scr_written")
        st_loaded = [sem(f"st_loaded{n}") for n in range(2)]
        sm_ready, sm_done = sem("sm_ready"), sem("sm_done")
        mxT_ready, mx_ready, mxlo_ready = sem("mxT_ready"), sem("mx_ready"), sem("mxlo_ready")
        mx_loaded = [sem(f"mx_loaded{n}") for n in range(2)]
        st_ready, exp_done, prob_ready = sem("st_ready"), sem("exp_done"), sem("prob_ready")
        pv_ready, oT_ready = sem("pv_ready"), sem("oT_ready")
        otr_ready, rec_ready, onorm_ready = sem("otr_ready"), sem("rec_ready"), sem("onorm_ready")
        xadd_done = sem("xadd_done")
        out_done = sem("out_done")
        dve_passed, pe_passed, pool_passed = sem("dve_passed"), sem("pe_passed"), sem("pool_passed")

        N_SCR, N_ST = 4, 12
        NG = NB * G

        block = ctx.enter_context(nc.Block())

        @block.sync
        def _(sp):
            w_up_v = W_up.rearrange("(n p) d -> p n d", p=P)
            w_gate_v = W_gate.rearrange("(n p) d -> p n d", p=P)
            w_down_v = W_down.rearrange("(t p) e -> p t e", p=P)
            sp.dma_start(w_raw[:, 0, :].rearrange("p (n d) -> p n d", d=D), w_up_v).then_inc(ld_w[0], 16)
            sp.dma_start(x[:, 0:TT, :], x_dram[:, 0:TT, :]).then_inc(ld_x0, 16)
            sp.dma_start(w_raw[:, 1, :].rearrange("p (n d) -> p n d", d=D), w_gate_v).then_inc(ld_w[1], 16)
            sp.dma_start(w_raw[:, 2, :].rearrange("p (t e) -> p t e", e=F), w_down_v).then_inc(ld_w[2], 16)
            sp.dma_start(x[:, TT:2 * TT, :], x_dram[:, TT:2 * TT, :]).then_inc(ld_x1, 16)
            sp.dma_start(x[:, 2 * TT:NT, :], x_dram[:, 2 * TT:NT, :]).then_inc(ld_xr, 16)
            for t in range(ND):
                rows = slice(t * P, (t + 1) * P)
                sp.dma_start(wq[:, t, :].rearrange("p (h d) -> p h d", d=DH),
                             Wq[:, rows, :].rearrange("h e d -> e h d")).then_inc(ld_attn, 16)
                sp.dma_start(wkv[:, t, 0:G * DH].rearrange("p (g d) -> p g d", d=DH),
                             Wv[:, rows, :].rearrange("g e d -> e g d")).then_inc(ld_attn, 16)
                sp.dma_start(wkv[:, t, G * DH:P].rearrange("p (g d) -> p g d", d=DH),
                             Wk[:, rows, :].rearrange("g e d -> e g d")).then_inc(ld_attn, 16)
            for t in range(2):
                sp.dma_start(bq_col[:, t:t + 1],
                             bq[t * H // 2:(t + 1) * H // 2, :].rearrange("h (d a) -> (h d) a", a=1)).then_inc(ld_attn, 16)
            sp.dma_start(bkv_col[0:G * DH, :], bv.rearrange("g (d a) -> (g d) a", a=1)).then_inc(ld_attn, 16)
            sp.dma_start(bkv_col[G * DH:P, :], bk.rearrange("g (d a) -> (g d) a", a=1)).then_inc(ld_attn, 16)

            def write_scratch(c, par):
                sp.wait_ge(qkv_lo, 3 * c + 3)
                for part, k_part, q_part in ((0, k_hi, q_hi), (1, k_lo, q_lo)):
                    sp.dma_start(k_scr[par, part].rearrange("g d t -> (g d) t"),
                                 k_part[G * DH:P, :]).then_inc(scr_written, 16)
                    sp.dma_start(q_scr[par, part].rearrange("(m h) d t -> (h d) m t", m=2),
                                 q_part[:, :, :]).then_inc(scr_written, 16)

            def read_scratch(c, par):
                sp.wait_ge(scr_written, 16 * N_SCR * (c + 1))
                for n, (q_part, k_part) in enumerate(((0, 0), (1, 0), (0, 1), (1, 1))):
                    rows = slice(n * DH, (n + 1) * DH)
                    for dst, scr, part in ((k_mx, k_scr, k_part), (k_st, k_scr, k_part), (q_st, q_scr, q_part)):
                        sp.dma_start(dst[rows, par, :, :],
                                     scr[par, part].rearrange("h d t -> d h t")).then_inc(st_loaded[par], 16)

            def load_max(b, k, half):
                par, seq = k // 2 % 2, k % 2
                sp.wait_ge(mxlo_ready, 2 * b + half + 1)
                heads, cols = slice(half * HH, (half + 1) * HH), slice(seq * S, (seq + 1) * S)
                sp.dma_start(q_st[64:65, par, heads, cols], mx_hi[:, half, :]).then_inc(mx_loaded[half], 16)
                sp.dma_start(q_st[65:66, par, heads, cols], mx_lo[:, half, :]).then_inc(mx_loaded[half], 16)

            def attention_pair(pair, last):
                c0 = 2 * pair
                for k in range(4):
                    b, odd = 2 * c0 + k, k % 2
                    c, par = c0 + k // 2, k // 2
                    for g in range(G):
                        if g in (0, 2) and not (last and k == 3):
                            load_max(b + 1, k + 1, g // 2)
                        if odd and g == 1 and not last:
                            write_scratch(c + 2, par)
                        if odd and g == 2 and not last:
                            sp.wait_ge(st_ready, 3 * G * (b + 1))
                            read_scratch(c + 2, par)

            sp.wait_ge(const_ready, 3)
            write_scratch(0, 0)
            read_scratch(0, 0)
            write_scratch(1, 1)
            read_scratch(1, 1)
            load_max(0, 0, 0)
            load_max(0, 0, 1)
            with sp.Fori(0, NC // 2 - 1) as i:
                attention_pair(i, False)
            attention_pair(NC // 2 - 1, True)
            for c in range(NC):
                sp.wait_ge(res_done, 2 + NT + TT * (c + 1))
                sp.dma_start(out_dram[:, TT * c:TT * (c + 1), :],
                             x[:, TT * c:TT * (c + 1), :]).then_inc(out_done, 16)
            sp.wait_ge(out_done, 16 * NC)

        @block.gpsimd
        def _(pool):
            steps = [0]

            def step(ins):
                steps[0] += 1
                ins.then_inc(pool_self, 1)
                pool.wait_ge(pool_self, steps[0])

            step(pool.memset(ident32[:, :], 0.0))
            step(pool.affine_select(out=ident32[:, :], in_=ident32[:, :], compare_op=ALU.not_equal, fill=1.0,
                                    base=0, pattern=[[-1, P]], channel_multiplier=1))
            step(pool.tensor_copy(ident16[:, :], ident32[:, :]))
            pool.memset(ones[:, :], 1.0).then_inc(const_ready, 1)
            pool.wait_ge(const_ready, 1)
            step(pool.memset(mask[:, :], 0.0))
            step(pool.affine_select(out=mask[:, P:S], in_=mask[:, P:S], compare_op=ALU.is_ge, fill=MASKED,
                                    base=0, pattern=[[-1, P]], channel_multiplier=1))
            step(pool.memset(val[:, :, :, :, :], 0.0))
            pool.memset(val[:, :, :, :, DH:DH + 1], 1.0).then_inc(const_ready, 1)
            pool.wait_ge(const_ready, 2)
            step(pool.memset(k_st[64:P, :, :, :], 0.0))
            step(pool.memset(k_st[64:66, :, :, :], MAX_UNIT))
            step(pool.memset(k_mx[64:P, :, :, :], 0.0))
            pool.memset(q_st[64:P, :, :, :].bitcast(U32), 0).then_inc(const_ready, 1)
            pool.wait_ge(const_ready, 3)
            pool.memset(o_norm[:, :, :], 0.0).then_inc(xadd_done, 2)
            pool.wait_ge(xadd_done, 2)

            def causal(n, par):
                pool.wait_ge(exp_done, 3 * n + 3)
                pool.sem_inc(pool_passed)
                early = prob[:, par, 0:2, :].rearrange("p i (h q) -> p (i h) q", q=S)[:, :, 0:P]
                late = prob[:, par, 2, :].rearrange("p (h q) -> p h q", q=P)
                pool.affine_select(out=early, in_=early, compare_op=ALU.is_ge, fill=0.0, base=0,
                                   pattern=[[0, HPG], [1, P]], channel_multiplier=-1)
                pool.affine_select(out=late, in_=late, compare_op=ALU.is_ge, fill=0.0, base=0,
                                   pattern=[[0, HPG], [1, P]], channel_multiplier=-1).then_inc(prob_ready, 1)

            def max_rest(b, half):
                pool.wait_ge(mx_ready, 2 * b + half + 1)
                if not isinstance(b, int) or b > 0:
                    pool.wait_ge(mx_loaded[half], 32 * b)
                pool.tensor_tensor(mx_lo[:, half, :], mx_32[:, half, :], mx_hi[:, half, :],
                                   ALU.subtract).then_inc(mxlo_ready, 1)

            def attention_pair(pair, last):
                c0 = 2 * pair
                for k in range(4):
                    b, odd = 2 * c0 + k, k % 2
                    c = c0 + k // 2
                    for g in range(G):
                        end = last and k == 3
                        if odd and g in (2, 3):
                            add_output(b - 1, g - 2, 3 - g)
                        if not (end and g == 3):
                            causal(4 * b + g + 1, (g + 1) % 2)
                        if g in (0, 2) and not end:
                            max_rest(b + 1, g // 2)
                        if not odd and g == 3 and not last:
                            centre_chunk(NC + c + 3, (TT * (c + 3)) % NT)
                        if odd and g == 2 and not last:
                            scale_chunk(NC + c + 3)
                    if odd:
                        add_output(b, 0, 0)
                        add_output(b, 1, 1)

            def add_output(b, n, qt):
                pool.wait_ge(onorm_ready, 2 * b + n + 3)
                tile = x[:, 2 * b + qt, :]
                pool.tensor_tensor(tile, tile, o_norm[:, qt, :], ALU.add).then_inc(xadd_done, 1)

            def centre_chunk(q, t0):
                pool.wait_ge(ln_mv, q + 1)
                pool.wait_ge(tr_ready, 2 * q)
                pool.tensor_tensor(xn[:, :, :], x[:, bass.ds(t0, TT), :], mv[:, :, 0:1].to_broadcast([P, TT, D]),
                                   ALU.subtract).then_inc(xn_centred, 1)

            def scale_chunk(q):
                pool.wait_ge(ln_rstd, RSTD_STEPS * (q + 1))
                pool.wait_ge(xn_centred, q)
                pool.tensor_tensor(xn[:, :, :], xn[:, :, :], rstd[:, :].unsqueeze(2).to_broadcast([P, TT, D]),
                                   ALU.mult).then_inc(xn_ready, 1)

            def normed_chunk(q, t0):
                centre_chunk(q, t0)
                scale_chunk(q)

            normed_chunk(1, TT)
            pool.wait_ge(most_ready, 1)
            pool.partition_all_reduce(qk_bound[:, :], qk_most[:, :], P, RMAX).then_inc(bound_ready, 1)
            with pool.Fori(2, NC) as c:
                normed_chunk(c, TT * c)
            normed_chunk(NC, 0)
            normed_chunk(NC + 1, TT)
            max_rest(0, 0)
            max_rest(0, 1)
            normed_chunk(NC + 2, 2 * TT)
            causal(0, 0)
            with pool.Fori(0, NC // 2 - 1) as i:
                attention_pair(i, False)
            attention_pair(NC // 2 - 1, True)
            with pool.Fori(1, NC) as c:
                normed_chunk(2 * NC + c, TT * c)

        @block.scalar
        def _(act):
            def abs_sum(m):
                act.wait_ge(ld_w[m], 16)
                if m:
                    act.wait_ge(abs_ready, m)
                act.activation(w_abs, w_raw[:, m, :], ACT.Abs, accum_out=w_sum[:, m:m + 1]).then_inc(abs_ready, 1)

            def copy_weights(m):
                dst = (wT_up[:, :, :], wT_gate[:, :, :],
                       wT_down[:, :, :].rearrange("p (a n) d -> p a (n d)", a=2))[m]
                for t in range(2):
                    act.wait_ge(wtr_ready, 2 * m + t + 1)
                    act.activation(dst[:, t, :], bank16[2 * m + t], ACT.Copy).then_inc(wT_ready, 1)

            def x_high(n, q, par, d):
                act.wait_ge(tr_ready, 2 * q + d + 1)
                act.activation(xh[:, par, d, :], TR[d][:, :], ACT.Copy).then_inc(xh_ready, 1)

            def feed_forward(ph):
                def chunk(c, par, nxt, tail=False):
                    first = ph == 0 and isinstance(c, int) and c == 0
                    for e in range(NE):
                        s = 64 * ph + NE * c + e
                        act.wait_ge(u_ready, s + 1)
                        if not (isinstance(s, int) and s < 2):
                            act.wait_ge(hid_ready, s - 1)
                        act.activation(silu[:, e % 2, :], U[e % 2][:, :], ACT.Silu,
                                       scale=w_scale[:, 0:1]).then_inc(silu_ready, 1)
                        if nxt and e == 6:
                            x_high(NC * ph + c + 1, 2 * NC * ph + c + 1, 1 - par, 0)
                        act.wait_ge(hid_ready, s + 1)
                        act.activation(hh[:, par, e, :], hid[:, e % 2, :], ACT.Copy).then_inc(hh_ready, 1)
                        if nxt and e == 6:
                            x_high(NC * ph + c + 1, 2 * NC * ph + c + 1, 1 - par, 1)
                        if tail and e == 6:
                            xT_copy(0)
                        if tail and e == 7:
                            key_high(0)
                            values(0)
                            query_high(0, 0)
                        if first and e == 6:
                            copy_weights(2)
                if ph == 0:
                    for d in range(ND):
                        x_high(0, 0, 0, d)
                    copy_weights(1)
                    abs_sum(2)
                chunk(0, 0, True)
                with act.Fori(0, NC // 2 - 1) as i:
                    chunk(2 * i + 1, 1, True)
                    chunk(2 * i + 2, 0, True)
                chunk(NC - 1, 1, False, ph == 0)

            def xT_copy(c, tiles=range(ND)):
                for d in tiles:
                    act.wait_ge(tr_ready, 2 * (NC + c) + d + 1)
                    act.activation(xT[:, d, :], MI[d][:, :], ACT.Copy).then_inc(xT_ready, 1)

            def key_high(c):
                act.wait_ge(qkv_ready, 3 * c + 1)
                if isinstance(c, int) and c == 0:
                    act.wait_ge(attn_w_ready, 3)
                else:
                    act.wait_ge(scr_written, 16 * N_SCR * c)
                act.activation(k_hi[G * DH:P, :], MI[0][G * DH:P, :], ACT.Identity,
                               bias=bkv_col[G * DH:P, :]).then_inc(qkv_hi, 1)

            def values(c):
                act.wait_ge(qkv_ready, 3 * c + 1)
                act.activation(vT[:, :], MI[0][0:G * DH, :], ACT.Identity, bias=bkv_col[0:G * DH, :]).then_inc(vT_ready, 1)

            def query_high(c, m):
                act.wait_ge(qkv_ready, 3 * c + m + 2)
                act.activation(q_hi[:, m, :], MI[1 - m][:, :], ACT.Identity,
                               bias=bq_col[:, m:m + 1]).then_inc(qkv_hi, 1)

            def val_copy(c, par):
                act.wait_ge(vtr_ready, c + 1)
                act.activation(val[:, par, :, :, 0:DH],
                               MI[1][:, 0:TT * G * DH].rearrange("p (t g d) -> p t g d", t=TT, g=G),
                               ACT.Copy).then_inc(val_ready, 1)

            def max_copy(b, half):
                act.wait_ge(mxT_ready, 2 * b + half + 1)
                if not (isinstance(b, int) and b == 0):
                    act.wait_ge(mx_loaded[half], 32 * b)
                act.activation(mx_hi[:, half, :], MT[0:HH, :], ACT.Copy, scale=-1.0 / MAX_UNIT)
                act.activation(mx_32[:, half, :], MT[0:HH, :], ACT.Copy,
                               scale=-1.0 / MAX_UNIT).then_inc(mx_ready, 1)

            def exps(n, place, parts):
                for i in parts:
                    act.wait_ge(st_ready, 3 * n + i + 1)
                    act.activation(prob[:, place % 2, i, :], ST[(3 * place + i) % 2][:, :], ACT.Exp,
                                   scale=qk_scale[:, 4:5]).then_inc(exp_done, 1)

            def attention_pair(pair, last):
                c0 = 2 * pair
                for k in range(4):
                    b, odd = 2 * c0 + k, k % 2
                    c, par = c0 + k // 2, k // 2
                    for g in range(G):
                        n, end = 4 * b + g, last and k == 3
                        ahead = (n + 1, 4 * k + g + 1)
                        if not (end and g == 3):
                            exps(*ahead, range(0, 1))
                        if not last:
                            if not odd and g == 1:
                                xT_copy(c + 2, range(1, 2))
                            if not odd and g == 2:
                                key_high(c + 2)
                            if not odd and g == 3:
                                query_high(c + 2, 0)
                            if odd and g == 0:
                                query_high(c + 2, 1)
                        if not (end and g == 3):
                            exps(*ahead, range(1, 3))
                        act.wait_ge(pv_ready, n + 1)
                        if g in (0, 2) and not end:
                            max_copy(b + 1, g // 2)
                        act.activation(oT[:, odd, g, :], PV[:, 0:S], ACT.Copy).then_inc(oT_ready, 1)
                        if odd and g == 3 and not last:
                            val_copy(c + 2, par)
                        if not odd and g == 0 and not last:
                            xT_copy(c + 2, range(0, 1))
                        if not odd and g == 2 and not last:
                            values(c + 2)
                        if last and k == 2 and g == 0:
                            for d in range(ND):
                                x_high(NC, 2 * NC, 0, d)

            def attention():
                query_high(0, 1)
                val_copy(0, 0)
                xT_copy(1)
                key_high(1)
                values(1)
                query_high(1, 0)
                query_high(1, 1)
                max_copy(0, 0)
                val_copy(1, 1)
                max_copy(0, 1)
                act.sem_inc(oT_ready)
                exps(0, 0, range(3))
                with act.Fori(0, NC // 2 - 1) as i:
                    attention_pair(i, False)
                attention_pair(NC // 2 - 1, True)

            abs_sum(0)
            abs_sum(1)
            copy_weights(0)
            feed_forward(0)
            attention()
            feed_forward(1)

        @block.vector
        def _(dve):
            steps = [0]

            def step(ins):
                steps[0] += 1
                ins.then_inc(dve_self, 1)
                dve.wait_ge(dve_self, steps[0])

            def scale_of(m):
                dve.wait_ge(wsum_ready, m + 1)
                step(dve.tensor_scalar(w_scale[:, m:m + 1], ACC[m % 2][:, 0:1], 1.0 / (F * D), QUANT_EPS,
                                       ALU.mult, ALU.add))
                dve.tensor_scalar(w_thr[:, m, 0:1], w_scale[:, m:m + 1], 0.5, None, ALU.mult)
                step(dve.tensor_scalar(w_thr[:, m, 1:2], w_scale[:, m:m + 1], -0.5, None, ALU.mult))

            def ternary(m, quarters=range(4)):
                if m and 0 in quarters:
                    dve.wait_ge(wtr_ready, 2 * m)
                size = NE * D // 4
                cols = slice(quarters[0] * size, (quarters[-1] + 1) * size)
                step(dve.tensor_scalar(w_neg[:, cols], w_raw[:, m, cols], w_thr[:, m, 1:2], None, ALU.is_lt))
                dve.scalar_tensor_tensor(out=w_tern[:, cols], in0=w_raw[:, m, cols], scalar=w_thr[:, m, 0:1],
                                         in1=w_neg[:, cols], op0=ALU.is_gt,
                                         op1=ALU.subtract).then_inc(tern_ready, len(quarters))

            def ln_stats_of(q, t0, tiles):
                for t in tiles:
                    ins = dve.bn_stats(stats[:, t, :], x[:, t0 + t, :])
                if TT - 1 in tiles:
                    ins.then_inc(ln_stats, 1)

            def ln_moments(q):
                dve.wait_ge(ln_stats, q + 1)
                if not (isinstance(q, int) and q == 0):
                    dve.wait_ge(xn_ready, q)
                dve.sem_inc(dve_passed)
                for t in range(TT):
                    ins = dve.bn_aggr(mv[:, t, :], stats[:, t, :])
                ins.then_inc(ln_mv, 1)

            def ln_rstd_steps(q, steps):
                for i in steps:
                    if i == 0:
                        dve.wait_ge(ln_mv, q + 1)
                        ins = dve.tensor_scalar(var[:, :], mv[:, :, 1], LN_EPS, None, ALU.add)
                    else:
                        dve.wait_ge(ln_rstd, RSTD_STEPS * q + i)
                    if i == 1:
                        ins = dve.tensor_scalar(rstd[:, :].bitcast(U32), var[:, :].bitcast(U32), 1, None,
                                                ALU.logical_shift_right)
                    elif i == 2:
                        ins = dve.tensor_scalar(rstd[:, :].bitcast(I32), rstd[:, :].bitcast(I32), -1.0,
                                                float(RSQRT_GUESS), ALU.mult, ALU.add)
                    elif i and i % 3 == 0:
                        ins = dve.tensor_tensor(newton[:, 0, :], var[:, :], rstd[:, :], ALU.mult)
                    elif i and i % 3 == 1:
                        ins = dve.scalar_tensor_tensor(out=newton[:, 1, :], in0=newton[:, 0, :], scalar=-0.5,
                                                       in1=rstd[:, :], op0=ALU.mult, op1=ALU.mult)
                    elif i:
                        ins = dve.scalar_tensor_tensor(out=rstd[:, :], in0=newton[:, 1, :], scalar=1.5,
                                                       in1=rstd[:, :], op0=ALU.add, op1=ALU.mult)
                    ins.then_inc(ln_rstd, 1)

            def ln_whole(q, t0):
                ln_stats_of(q, t0, range(TT))
                ln_moments(q)
                ln_rstd_steps(q, range(RSTD_STEPS))
                ln_4(q, t0)

            def ln_4(q, t0):
                dve.wait_ge(ln_rstd, RSTD_STEPS * (q + 1))
                if not (isinstance(q, int) and q == 0):
                    dve.wait_ge(tr_ready, 2 * q)
                for t in range(TT):
                    ins = dve.tensor_scalar(xn[:, t, :], x[:, t0 + t, :], mv[:, t, 0:1], rstd[:, t:t + 1],
                                            ALU.subtract, ALU.mult)
                ins.then_inc(xn_ready, 1)

            def x_low(n, par, d):
                dve.wait_ge(xh_ready, 2 * n + d + 1)
                dve.tensor_tensor(xl[:, par, d, :], TR[d][:, :], xh[:, par, d, :],
                                  ALU.subtract).then_inc(xl_ready, 1)

            def feed_forward(ph):
                def chunk(c, par, down, nxt, tail=False):
                    q = 2 * NC * ph + c + 1
                    t0 = 0 if tail else TT * (c + 1)
                    first = ph == 0 and isinstance(c, int) and c == 0
                    for e in range(NE):
                        s = 64 * ph + NE * c + e
                        dve.wait_ge(silu_ready, s + 1)
                        dve.wait_ge(g_ready, s + 1)
                        dve.scalar_tensor_tensor(out=hid[:, e % 2, :], in0=silu[:, e % 2, :], scalar=h_unit[:, 0:1],
                                                 in1=GT[e % 2][:, :], op0=ALU.mult, op1=ALU.mult).then_inc(hid_ready, 1)
                        if nxt or tail:
                            if e == 0:
                                if tail:
                                    dve.wait_ge(res_done, 2 + 2 * TT)
                                elif ph:
                                    dve.wait_ge(xadd_done, 2 + TT * (c + 2))
                                else:
                                    dve.wait_ge(ld_x1 if first else ld_xr, 16)
                                ln_stats_of(q, t0, range(0, 2))
                            if e == 1:
                                ln_stats_of(q, t0, range(2, 4))
                                ln_moments(q)
                            if e in (2, 3):
                                ln_rstd_steps(q, range(6 * e - 12, 6 * e - 8))
                        if tail and e == 1:
                            scale_projections()
                        if first and e in (1, 2, 3, 4):
                            if e == 1:
                                scale_of(2)
                            ternary(2, range(e - 1, e))
                            if e == 4:
                                step(dve.tensor_tensor(y_scale[:, 0:1], w_scale[:, 0:1], w_scale[:, 1:2], ALU.mult))
                                step(dve.tensor_tensor(y_scale[:, 1:2], y_scale[:, 0:1], w_scale[:, 2:3], ALU.mult))
                        if tail:
                            if e in (4, 5):
                                ln_stats_of(q + 1, TT, range(2 * e - 8, 2 * e - 6))
                            if e == 6:
                                ln_moments(q + 1)
                            if e in (6, 7):
                                ln_rstd_steps(q + 1, range(6 * e - 36, 6 * e - 30))
                        dve.wait_ge(hh_ready, s + 1)
                        dve.tensor_tensor(hl[:, par, e, :], hid[:, e % 2, :], hh[:, par, e, :],
                                          ALU.subtract).then_inc(hl_ready, 1)
                        if (nxt or tail) and e in (2, 3):
                            ln_rstd_steps(q, range(6 * e - 8, 6 * e - 6))
                        if nxt and e == 6:
                            for d in range(ND):
                                x_low(NC * ph + c + 1, 1 - par, d)
                        if down and e % 2:
                            residual(c - 1, e // 2)

                def residual(c, t):
                    dve.wait_ge(acc_ready, NT * ph + TT * c + t + 1)
                    tile = x[:, TT * c + t, :]
                    dve.scalar_tensor_tensor(out=tile, in0=ACC[t % 2][:, 0:D], scalar=y_scale[:, 1:2], in1=tile,
                                             op0=ALU.mult, op1=ALU.add).then_inc(res_done, 1)

                if ph == 0:
                    dve.wait_ge(ld_x0, 16)
                    ln_whole(0, 0)
                    scale_of(1)
                    ternary(1)
                    for d in range(ND):
                        x_low(0, 0, d)
                chunk(0, 0, False, True)
                if ph == 0:
                    projection_ends()
                with dve.Fori(0, NC // 2 - 1) as i:
                    chunk(2 * i + 1, 1, True, True)
                    chunk(2 * i + 2, 0, True, True)
                chunk(NC - 1, 1, True, False, ph == 0)
                if ph == 0:
                    key_low(0)
                    residual(NC - 1, 0)
                    query_low(0, 0)
                    residual(NC - 1, 1)
                    query_low(0, 1)
                    residual(NC - 1, 2)
                    residual(NC - 1, 3)
                else:
                    for t in range(TT):
                        residual(NC - 1, t)

            def projection_ends():
                dve.wait_ge(ld_attn, 16 * 10)
                step(dve.memset(qk_ends[:, :, :], 0.0))
                for n, op in enumerate((ALU.max, ALU.min)):
                    dve.tensor_reduce(qk_ends[:, n, 0:1], wq[:, :, :].rearrange("p t n -> p (t n)"), AXX, op)
                    dve.tensor_reduce(qk_ends[:, n, 1:2], wkv[:, :, G * DH:P], mybir.AxisListType.XY, op)
                    dve.tensor_reduce(qk_ends[:, n, 2:3], bq_col[:, :], AXX, op)
                    ins = dve.tensor_copy(qk_ends[G * DH:P, n, 3:4], bkv_col[G * DH:P, :])
                step(ins)
                dve.scalar_tensor_tensor(out=qk_most[:, :], in0=qk_ends[:, 1, :], scalar=-1.0, in1=qk_ends[:, 0, :],
                                         op0=ALU.mult, op1=ALU.max).then_inc(most_ready, 1)

            def scale_projections():
                dve.wait_ge(bound_ready, 1)
                step(dve.scalar_tensor_tensor(out=qk_scale[:, 0:2], in0=qk_bound[:, 0:2], scalar=float(D),
                                              in1=qk_bound[:, 2:4], op0=ALU.mult, op1=ALU.add))
                step(dve.tensor_scalar(qk_scale[:, 0:2], qk_scale[:, 0:2], 1e-12, None, ALU.max))
                step(dve.reciprocal(qk_scale[:, 2:4], qk_scale[:, 0:2]))
                step(dve.tensor_scalar(qk_scale[:, 2:4].bitcast(U32), qk_scale[:, 2:4].bitcast(U32), EXPONENT_BITS, None,
                                       ALU.bitwise_and))
                step(dve.tensor_scalar(qk_scale[:, 2:4], qk_scale[:, 2:4], QK_BOUND, None, ALU.mult))
                step(dve.tensor_tensor(qk_scale[:, 5:6], qk_scale[:, 2:3], qk_scale[:, 3:4], ALU.mult))
                step(dve.reciprocal(qk_scale[:, 6:7], qk_scale[:, 5:6]))
                dve.tensor_scalar(qk_scale[:, 4:5], qk_scale[:, 6:7], float(DH) ** -0.5, None,
                                  ALU.mult).then_inc(attn_w_ready, 1)
                all_q = wq[:, :, :].rearrange("p t n -> p (t n)")
                dve.tensor_scalar(all_q, all_q, qk_scale[:, 2:3], None, ALU.mult)
                dve.tensor_scalar(wkv[:, :, G * DH:P], wkv[:, :, G * DH:P], qk_scale[:, 3:4], None,
                                  ALU.mult).then_inc(attn_w_ready, 1)
                dve.tensor_scalar(bq_col[:, :], bq_col[:, :], qk_scale[:, 2:3], None, ALU.mult)
                dve.tensor_scalar(bkv_col[G * DH:P, :], bkv_col[G * DH:P, :], qk_scale[G * DH:P, 3:4], None,
                                  ALU.mult).then_inc(attn_w_ready, 1)

            def key_low(c):
                dve.wait_ge(qkv_hi, 3 * c + 1)
                dve.scalar_tensor_tensor(out=k_lo[G * DH:P, :], in0=MI[0][G * DH:P, :], scalar=bkv_col[G * DH:P, :],
                                         in1=k_hi[G * DH:P, :], op0=ALU.add, op1=ALU.subtract).then_inc(qkv_lo, 1)

            def query_low(c, m):
                dve.wait_ge(qkv_hi, 3 * c + m + 2)
                dve.scalar_tensor_tensor(out=q_lo[:, m, :], in0=MI[1 - m][:, :], scalar=bq_col[:, m:m + 1],
                                         in1=q_hi[:, m, :], op0=ALU.add, op1=ALU.subtract).then_inc(qkv_lo, 1)

            def row_max(n, seq_par, g, i, norm, steps):
                dve.wait_ge(sm_ready, 3 * n + i + 1)
                dve.sem_inc(dve_passed)
                heads = range(HPG) if i == 2 else range(2 * i, 2 * i + 2)
                size, qt = (P, 0) if i == 2 else (S, 1)
                for j in heads:
                    cols = slice((j - heads[0]) * size, (j - heads[0] + 1) * size)
                    h = HPG * g + j
                    ins = dve.tensor_tensor_reduce(sm_out[:, i, cols], SM[i][:, cols], mask[:, S - size:S], 1.0, MASKED,
                                                   ALU.add, ALU.max, rowmax[:, seq_par, qt, h:h + 1])
                    if j == heads[-1]:
                        ins.then_inc(sm_done, 1)
                    else:
                        at = j // 2 if i < 2 else j // 2 + 2
                        if i < 2 or j != 1:
                            ln_rstd_steps(norm, steps[at:at + 1])

            def normalise(b, n, qt):
                heads = MI[qt][:, :].rearrange("p (h w) -> p h w", w=VW)
                dve.wait_ge(otr_ready, 2 * b + n + 1)
                dve.reciprocal(o_rec[:, qt, :], heads[:, :, DH]).then_inc(rec_ready, 1)
                dve.wait_ge(rec_ready, 2 * b + n + 1)
                dve.wait_ge(xadd_done, 2 * b + 2 - n)
                dve.tensor_tensor(o_norm[:, qt, :].rearrange("p (h d) -> p h d", d=DH), heads[:, :, 0:DH],
                                  o_rec[:, qt, :].unsqueeze(2).to_broadcast([P, H, DH]),
                                  ALU.mult).then_inc(onorm_ready, 1)

            def attention_pair(pair, last):
                c0 = 2 * pair
                for k in range(4):
                    b, odd = 2 * c0 + k, k % 2
                    c = c0 + k // 2
                    q = NC + c + 3
                    for g in range(G):
                        lead = (4 * b + g + 6, (k + (g + 6) // 4) % 2, (g + 2) % 4)
                        ahead = not (last and (k == 3 or (k == 2 and g >= 2)))
                        norm = () if last else {(0, 3): range(0, 4), (1, 0): range(4, 8),
                                                (1, 1): range(8, 12)}.get((odd, g), ())
                        for i in range(3):
                            if ahead:
                                row_max(*lead, i, q, norm)
                            if not odd and not last:
                                if g == 1 and i == 0:
                                    dve.wait_ge(xadd_done, TT * c + 1)
                                if g == 1 or (g == 2 and i == 0):
                                    t = i if g == 1 else 3
                                    ln_stats_of(q, (TT * (c + 3)) % NT, range(t, t + 1))
                                if g == 2 and i == 1:
                                    ln_moments(q)
                                if g == 2 and i == 2:
                                    key_low(c + 2)
                                if g == 3 and i == 2:
                                    query_low(c + 2, 0)
                            if odd and g == 0 and i == 2 and not last:
                                query_low(c + 2, 1)
                            if last and k == 2 and g == 1 and i < ND:
                                x_low(NC, 0, i)
                            if odd and g in (1, 2) and i == 0:
                                normalise(b - 1, g - 1, 2 - g)
                    if odd:
                        normalise(b, 0, 0)
                        normalise(b, 1, 1)

            def attention():
                key_low(1)
                dve.wait_ge(const_ready, 2)
                q = NC + 2
                for n in range(6):
                    for i in range(3):
                        row_max(n, n // G, n % G, i, q, range(4 * (n - 2), 4 * (n - 1)) if 2 <= n < 5 else ())
                        if n < 2 and 3 * n + i < TT:
                            ln_stats_of(q, 2 * TT, range(3 * n + i, 3 * n + i + 1))
                    if n == 1:
                        ln_moments(q)
                    if n < 2:
                        query_low(1, n)
                dve.wait_ge(val_ready, 2)
                dve.memset(o_rec[:, 0, 0:1], 0.0).then_inc(onorm_ready, 2)
                with dve.Fori(0, NC // 2 - 1) as i:
                    attention_pair(i, False)
                attention_pair(NC // 2 - 1, True)

            scale_of(0)
            step(dve.reciprocal(h_unit[:, 1:2], w_scale[:, 0:1]))
            step(dve.tensor_scalar(h_unit[:, 0:1], h_unit[:, 1:2], 0.5, None, ALU.mult))
            ternary(0)
            dve.memset(newton[:, :, :], 0.0).then_inc(res_done, 2)
            feed_forward(0)
            attention()
            feed_forward(1)

        @block.tensor
        def _(pe):
            def weight_sum(m):
                pe.wait_ge(abs_ready, m + 1)
                if m == 2:
                    pe.wait_ge(tern_ready, 1)
                pe.matmul(ACC[m % 2][:, 0:1], ones[:, :], w_sum[:, m:m + 1], start=True, stop=True).then_inc(wsum_ready, 1)

            def weight_transposes(m):
                pe.wait_ge(tern_ready, 4 * (m + 1))
                for t in range(2):
                    for j in range(8):
                        n, d = (j, t) if m < 2 else (4 * t + j // 2, j % 2)
                        at = n * D + d * P if m < 2 else d * F + n * P
                        ins = pe.transpose(bank16[2 * m + t][:, j * P:(j + 1) * P], w_tern[:, at:at + P], ident16[:, :])
                    ins.then_inc(wtr_ready, 1)

            def x_transposes(q, ready, tiles=range(ND)):
                pe.wait_ge(xn_ready, q + 1)
                for d in tiles:
                    for ready_sem, count in ready[d]:
                        pe.wait_ge(ready_sem, count)
                    for t in range(TT):
                        ins = pe.transpose(TR[d][:, t * P:(t + 1) * P], xn[:, t, d * P:(d + 1) * P], ident32[:, :])
                    ins.then_inc(tr_ready, 1)

            def feed_forward(ph):
                def up_gate(s, e, par):
                    for w, banks, done in ((wT_up, U, u_ready), (wT_gate, GT, g_ready)):
                        if not (isinstance(s, int) and s < 2):
                            pe.wait_ge(silu_ready if w is wT_up else hid_ready, s - 1)
                        for d in range(ND):
                            for part in (xh, xl):
                                ins = pe.matmul(banks[e % 2][:, :], w[:, d, e * P:(e + 1) * P], part[:, par, d, :],
                                                start=(d == 0 and part is xh), stop=(d == ND - 1 and part is xl))
                        ins.then_inc(done, 1)

                def down_half(c, par, t, half):
                    n = NT * ph + TT * c + t
                    if half == 0:
                        pe.wait_ge(res_done, n + 1)
                    for e in range(half * 4, half * 4 + 4):
                        for part in (hh, hl):
                            ins = pe.matmul(ACC[t % 2][:, 0:D], part[:, par, e, t * P:(t + 1) * P], wT_down[:, e, :],
                                            start=(e == 0 and part is hh), stop=(e == NE - 1 and part is hl))
                    if half:
                        ins.then_inc(acc_ready, 1)

                def chunk(c, par, down, nxt, tail=False):
                    n = NC * ph + c
                    pe.wait_ge(xl_ready, 2 * n + 2)
                    for e in range(NE):
                        s = 64 * ph + NE * c + e
                        up_gate(s, e, par)
                        if down:
                            if e < 2:
                                pe.wait_ge(hl_ready, s - 4 + 3 * e)
                            down_half(c - 1, 1 - par, e // 2, e % 2)
                        if (nxt or tail) and e == 5:
                            outputs_left = [[(onorm_ready, 2 * NB + 1)], [(onorm_ready, 2 * NB + 2)]]
                            x_transposes(2 * NC * ph + c + 1, outputs_left if ph and isinstance(c, int) and c == 0 else
                                         [[(xl_ready, 2 * n + 1)], [(xl_ready, 2 * n + 2)]])
                        if tail and e > 5:
                            project_both(0, e - 6)
                        if ph == 0 and isinstance(c, int) and c == 0:
                            if e == 0:
                                weight_sum(2)
                            if e == 5:
                                weight_transposes(2)

                if ph == 0:
                    x_transposes(0, [[], []])
                    weight_transposes(1)
                    pe.wait_ge(wT_ready, 4)
                chunk(0, 0, False, True)
                if ph == 0:
                    pe.wait_ge(wT_ready, 6)
                with pe.Fori(0, NC // 2 - 1) as i:
                    chunk(2 * i + 1, 1, True, True)
                    chunk(2 * i + 2, 0, True, True)
                chunk(NC - 1, 1, True, False, ph == 0)
                for t in range(TT):
                    for half in range(2):
                        if t == 0:
                            pe.wait_ge(hl_ready, 64 * (ph + 1) - 4 + 4 * half)
                        down_half(NC - 1, 1, t, half)
                    if ph == 0:
                        if t == 0:
                            project_both(0, 2)
                        if t == 1:
                            val_transposes(0, (qkv_lo, 2))
                        if t == 2:
                            x_transposes(NC + 1, [[(qkv_lo, 3)], [(val_ready, 1)]])
                        if t == 3:
                            project_both(1, 0)

            def project(c, m, part):
                half, d = part // ND, part % ND
                cols = slice(half * S, (half + 1) * S)
                if m == 0 and part < ND:
                    if isinstance(c, int) and c == 0:
                        pe.wait_ge(attn_w_ready, 3)
                    pe.wait_ge(xT_ready, 2 * c + 1 + part)
                if m == 2 and part == 0:
                    pe.wait_ge(vT_ready, c + 1)
                    pe.wait_ge(qkv_lo, 3 * c + 1)
                w = wkv[:, :, :] if m == 0 else wq[:, :, (m - 1) * P:m * P]
                ins = pe.matmul(MI[m % 2][:, cols], w[:, d, :], xT[:, d, cols], start=(d == 0), stop=(d == ND - 1))
                if part == 2 * ND - 1:
                    ins.then_inc(qkv_ready, 1)

            def project_both(c, m):
                for part in range(2 * ND):
                    project(c, m, part)

            def val_transposes(c, last_reader):
                pe.wait_ge(vT_ready, c + 1)
                pe.wait_ge(*last_reader)
                pe.sem_inc(pe_passed)
                for t in range(TT):
                    ins = pe.transpose(MI[1][:, t * G * DH:(t + 1) * G * DH], vT[:, t * P:(t + 1) * P],
                                       ident32[0:G * DH, 0:G * DH])
                ins.then_inc(vtr_ready, 1)

            def max_scores(n, k, g, parts=range(3)):
                par, at = k // 2 % 2, k % 2 * S
                for i in parts:
                    if not (isinstance(n, int) and n == 0):
                        pe.wait_ge(sm_done, 3 * n + i - 2)
                    heads = range(HPG) if i == 2 else range(2 * i, 2 * i + 2)
                    size, rows = (P, at) if i == 2 else (S, at + P)
                    for j in heads:
                        ins = pe.matmul(SM[i][:, (j - heads[0]) * size:(j - heads[0] + 1) * size],
                                        q_st[:, par, HPG * g + j, rows:rows + P], k_mx[:, par, g, at:at + size],
                                        start=True, stop=True)
                    ins.then_inc(sm_ready, 1)

            def max_transposes(b, k, half):
                pe.wait_ge(sm_done, 3 * (G * b + 2 * half + 2))
                if not (isinstance(b, int) and b == 0 and half == 0):
                    pe.wait_ge(mx_ready, 2 * b + half)
                for qt in range(QT):
                    ins = pe.transpose(MT[0:HH, qt * P:(qt + 1) * P], rowmax[:, k % 2, qt, half * HH:(half + 1) * HH],
                                       ident32[:, :])
                ins.then_inc(mxT_ready, 1)

            def scores(n, b, k, g, parts=range(3)):
                par, seq = k // 2 % 2, k % 2
                if g % 2 == 0 and 0 in parts:
                    pe.wait_ge(mx_loaded[g // 2], 32 * (b + 1))
                at, heads = seq * S, slice(HPG * g, HPG * (g + 1))
                for i in parts:
                    if not (isinstance(n, int) and n == 0 and i < 2):
                        pe.wait_ge(exp_done, 3 * n + i - 1)
                    if i < 2:
                        keys, queries = at, q_st[:, par, HPG * g + 2 * i:HPG * g + 2 * i + 2, at:at + S]
                    else:
                        keys, queries = at + P, q_st[:, par, heads, at + P:at + S]
                    pe.matmul(ST[(3 * (4 * k + g) + i) % 2][:, :], k_st[:, par, g, keys:keys + P], queries,
                              start=True, stop=True).then_inc(st_ready, 1)

            def outputs(n, k, g):
                par, seq = k // 2 % 2, k % 2
                pe.wait_ge(prob_ready, n + 1)
                for j in range(HPG):
                    rows = slice(VW * j, VW * (j + 1))
                    pe.matmul(PV[rows, 0:S], val[:, par, QT * seq, g, :],
                              prob[:, g % 2, j // 2, (j % 2) * S:(j % 2 + 1) * S], start=True, stop=False,
                              tile_position=(0, VW * j))
                for j in range(HPG):
                    rows = slice(VW * j, VW * (j + 1))
                    ins = pe.matmul(PV[rows, P:S], val[:, par, QT * seq + 1, g, :],
                                    prob[:, g % 2, 2, j * P:(j + 1) * P], start=False, stop=True,
                                    tile_position=(0, VW * j))
                ins.then_inc(pv_ready, 1)

            def output_transposes(b, k, qt, last_reader):
                pe.wait_ge(oT_ready, G * (b + 1) + 1)
                pe.wait_ge(*last_reader)
                for g in range(G):
                    ins = pe.transpose(MI[qt][:, g * P:(g + 1) * P], oT[:, k % 2, g, qt * P:(qt + 1) * P], ident32[:, :])
                ins.then_inc(otr_ready, 1)

            def attention_pair(pair, last):
                c0 = 2 * pair
                for k in range(4):
                    b, odd = 2 * c0 + k, k % 2
                    c, par = c0 + k // 2, k // 2
                    for g in range(G):
                        n, end = 4 * b + g, last and k == 3
                        lead = (n + 6, k + (g + 6) // 4, (g + 2) % 4)
                        ahead = not (end or (last and k == 2 and g >= 2))
                        def projection(place):
                            at = 4 * (4 * odd + g) + place - 5
                            if 0 <= at < 12 and not last:
                                project(c + 2, at // 4, at % 4)

                        following = (n + 1, b + (g + 1) // 4, k + (g + 1) // 4, (g + 1) % 4)
                        if ahead:
                            if not odd and g == 2:
                                pe.wait_ge(st_loaded[1 - par], 16 * N_ST * (pair + par + 1))
                            max_scores(*lead, range(0, 1))
                        projection(0)
                        if not (end and g == 3):
                            scores(*following, range(0, 1))
                        if ahead:
                            max_scores(*lead, range(1, 2))
                        projection(1)
                        if not (end and g == 3):
                            scores(*following, range(1, 2))
                        if ahead:
                            max_scores(*lead, range(2, 3))
                        projection(2)
                        nxt = 2 * NC if last else NC + c + 2
                        if not odd and g == 0 and not (last and k == 0):
                            x_transposes(nxt, [[(onorm_ready, 2 * b + 1)], []], range(0, 1))
                        if odd and g < 2:
                            output_transposes(b - 1, k - 1, 1 - g, (qkv_lo, 3 * (c + 2) + 2 + g) if not last else
                                              (onorm_ready, 2 * b - g) if k == 1 else (xl_ready, 2 * NC + 2 - g))
                        if not (end and g == 3):
                            scores(*following, range(2, 3))
                        if g == 0 and not odd:
                            pe.wait_ge(val_ready, c + 1)
                        pe.wait_ge(oT_ready, n + 1)
                        if g in (0, 2) and not end:
                            max_transposes(b + 1, k + 1, g // 2)
                        outputs(n, k, g)
                        if odd and g == 3 and not last:
                            val_transposes(c + 2, (onorm_ready, 2 * b + 1))
                        projection(3)
                        if not odd and g == 0 and not (last and k == 0):
                            x_transposes(nxt, [[], [(onorm_ready, 2 * b + 2)]], range(1, 2))
                        if odd and g == 3:
                            output_transposes(b, k, 0, (onorm_ready, 2 * b + 2))
                            output_transposes(b, k, 1, (onorm_ready, 2 * b + 1) if last else (val_ready, c + 3))

            def attention():
                pe.wait_ge(st_loaded[0], 16 * N_ST)
                for n in range(6):
                    max_scores(n, n // G, n % G)
                    if n < 2:
                        project_both(1, n + 1)
                    if n in (2, 4):
                        if n == 2:
                            pe.wait_ge(res_done, NT + 2)
                        max_transposes(0, 0, n // 2 - 1)
                    if n == 3:
                        val_transposes(1, (qkv_lo, 5))
                pe.wait_ge(val_ready, 2)
                scores(0, 0, 0, 0)
                with pe.Fori(0, NC // 2 - 1) as i:
                    attention_pair(i, False)
                attention_pair(NC // 2 - 1, True)

            pe.wait_ge(const_ready, 1)
            weight_sum(0)
            weight_sum(1)
            weight_transposes(0)
            feed_forward(0)
            attention()
            feed_forward(1)


_INS = ["L0_attn_x", "L0_attn_Wq", "L0_attn_bq", "L0_attn_Wk", "L0_attn_bk", "L0_attn_Wv", "L0_attn_bv",
        "L0_ffn_W_up", "L0_ffn_W_gate", "L0_ffn_W_down"]
_OUT = ((16, 256, 256), "float32")


def kernel(**inputs):
    import numpy as _np
    import concourse.bacc as _bacc
    from concourse import mybir as _mybir
    from concourse.bass_utils import run_bass_kernel_spmd as _run

    nc = _bacc.Bacc("TRN2", target_bir_lowering=False, num_devices=1)
    arrays, args = {}, []
    for name in _INS:
        a = _np.ascontiguousarray(inputs[name])
        arrays[f"in_{name}_dram"] = a
        args.append(nc.dram_tensor(f"in_{name}_dram", a.shape, _mybir.dt.from_np(a.dtype), kind="ExternalInput").ap())
    shape, dtype = _OUT
    out = nc.dram_tensor("out_0_dram", shape, _mybir.dt.from_np(_np.dtype(dtype)), kind="ExternalOutput").ap()
    macaron_block(nc, *args, out)
    r = _run(nc, [arrays], core_ids=[0])
    return r.results[0]["out_0_dram"]
```

```python
from contextlib import ExitStack

import concourse.bass as bass
from concourse import mybir

P = 128
ALU = mybir.AluOpType
ACT = mybir.ActivationFunctionType
AXX = mybir.AxisListType.X
F32 = mybir.dt.float32
F16 = mybir.dt.float16
U32 = mybir.dt.uint32
I32 = mybir.dt.int32
RMAX = bass.bass_isa.ReduceOp.max

LN_EPS = 1e-5
QUANT_EPS = 1e-8
MASKED = -1e30
QK_BOUND = 2048.0
MAX_UNIT = 4096.0
EXPONENT_BITS = 0x7F800000
RSQRT_GUESS = 0x5F3759DF
RSTD_STEPS = 12


def macaron_block(nc, heads, x_in, w_qkv, b_qkv, w_up_t, w_gate_t, w_down_t, out):
    NB, S, D = x_in.shape
    H, G, DH = heads
    HPG = H // G
    F = w_up_t.shape[1]
    ND = D // P
    NE = F // P
    TC = 512
    TT = TC // P
    NC = NB * S // TC
    BC = TC // S
    QT = S // P
    NT = NC * TT
    HH = H // 2
    VW = 32
    assert (ND, NE, TT, BC, QT, HPG, DH) == (2, 8, 4, 2, 2, 4, 16)

    x_dram = x_in.rearrange("b (t p) d -> p (b t) d", p=P)
    out_dram = out.rearrange("b (t p) d -> p (b t) d", p=P)
    q_scr = nc.dram_tensor("q_scratch", (2, 2, DH, H // 2, 2, TC), F16)
    k_scr = nc.dram_tensor("k_scratch", (2, 2, DH, G, TC), F16)

    with ExitStack() as ctx:
        def sb(name, shape, dt=F32):
            return ctx.enter_context(nc.sbuf_tensor(name, shape, dt))

        def sem(name):
            return ctx.enter_context(nc.semaphore(name))

        ident32 = sb("ident32", [P, P])
        ones = sb("ones", [P, P])
        mask = sb("mask", [P, S])
        shared = sb("shared", [P, 3 * NE * D])
        w_raw = shared[:, :].rearrange("p (m n) -> p m n", m=3)
        prob = shared[:, 0:6 * TC].rearrange("p (a i n) -> p a i n", a=2, i=3)
        oT = shared[:, 6 * TC:6 * TC + 2 * G * S].rearrange("p (a g n) -> p a g n", a=2, g=G)
        wT_up = sb("wT_up", [P, ND, F], F16)
        wT_gate = sb("wT_gate", [P, ND, F], F16)
        wT_down = sb("wT_down", [P, NE, D], F16)
        w_sum = sb("w_sum", [P, 3, 2])
        w_scale = sb("w_scale", [P, 3])
        w_thr = sb("w_thr", [P, 3, 2])
        h_unit = sb("h_unit", [P, 2])
        y_scale = sb("y_scale", [P, 2])
        wqkv = sb("wqkv", [P, ND, 3 * P])
        b_col = sb("b_col", [P, 3])
        qk_ends = sb("qk_ends", [P, 2, 4])
        qk_most = sb("qk_most", [P, 4])
        qk_bound = sb("qk_bound", [P, 4])
        qk_scale = sb("qk_scale", [P, 8])
        x = sb("x", [P, NT, D])
        stats = sb("stats", [P, TT, 6])
        mv = sb("mv", [P, TT, 2])
        var = sb("var", [P, TT])
        rstd = sb("rstd", [P, TT])
        newton = sb("newton", [P, 2, TT])
        xn = sb("xn", [P, TT, D])
        xnh, xnl = sb("xnh", [P, TT, D], F16), sb("xnl", [P, TT, D], F16)
        xh = sb("xh", [P, 2, TT, ND, P], F16)
        xl = sb("xl", [P, 2, TT, ND, P], F16)
        silu = sb("silu", [P, 2, TC])
        hid = sb("hid", [P, 4, TC])
        hh = sb("hh", [P, 2, NE, TC], F16)
        hl = sb("hl", [P, 2, NE, TC], F16)
        w_abs = hh[:, 1, 0:4, :].rearrange("p e n -> p (e n)")
        w_neg = [hl[:, 1, 0:2, :], hh[:, 1, 2:4, :], hl[:, 1, 2:4, :]]
        down_neg = hh[:, 1, 4:8, :].rearrange("p e n -> p (e n)")
        down_pos = hl[:, 1, 4:6, :].rearrange("p e n -> p (e n)")
        xT = sb("xT", [P, ND, TC])
        q_hl = sb("q_hl", [P, 2, 2, TC], F16)
        k_hl = sb("k_hl", [P, 2, TC], F16)
        vT = sb("vT", [G * DH, TC])
        q_st = sb("q_st", [P, 2, H, TC], F16)
        k_st = sb("k_st", [P, 2, G, TC], F16)
        val = sb("val", [P, 2, TT, G, VW])
        rowmax = sb("rowmax", [P, 2, QT, H])
        sm_out = sb("sm_out", [P, 3, 2 * S], F16)
        mx_hl = sb("mx_hl", [HH, 2, 2, S], F16)
        mx_32 = sb("mx_32", [HH, 2, S])
        o_rec = sb("o_rec", [P, 2, H])
        o_norm = sb("o_norm", [P, 2, D])

        bank = [ctx.enter_context(nc.psum_tensor(f"bank{i}", [P, 512], F32)) for i in range(8)]
        U, GT, ACC, TR = bank[0:2], bank[2:4], bank[4:6], bank[6:8]
        SM, ST, PV, MI = bank[0:3], bank[3:5], bank[5], bank[6:8]
        MT = PV[:, S:2 * S]
        FIRST_MT = ST[0][:, 0:S]

        ld_w = [[sem(f"ld_w{m}{half}") for half in range(2)] for m in range(3)]
        ld_x0, ld_x1, ld_xr = sem("ld_x0"), sem("ld_x1"), sem("ld_xr")
        ld_attn = sem("ld_attn")
        const_ready = sem("const_ready")
        pool_self = sem("pool_self")
        abs_ready = sem("abs_ready")
        wsum_ready = sem("wsum_ready")
        dve_self = sem("dve_self")
        tern_ready = sem("tern_ready")
        thr_ready = sem("thr_ready")
        neg_ready = sem("neg_ready")
        down_ready = sem("down_ready")
        most_ready = sem("most_ready")
        bound_ready = sem("bound_ready")
        attn_w_ready = sem("attn_w_ready")
        ln_stats, ln_mv, ln_rstd = sem("ln_stats"), sem("ln_mv"), sem("ln_rstd")
        xn_ready = sem("xn_ready")
        xn_centred = sem("xn_centred")
        tr_ready = sem("tr_ready")
        xnh_ready, xnl_ready = sem("xnh_ready"), sem("xnl_ready")
        xh_ready, xl_ready = sem("xh_ready"), sem("xl_ready")
        u_ready, g_ready = sem("u_ready"), sem("g_ready")
        silu_ready, hid_ready = sem("silu_ready"), sem("hid_ready")
        hh_ready, hl_ready = sem("hh_ready"), sem("hl_ready")
        acc_ready, res_done = sem("acc_ready"), sem("res_done")
        xT_ready = sem("xT_ready")
        qkv_ready = sem("qkv_ready")
        qkv_hi, qkv_lo = sem("qkv_hi"), sem("qkv_lo")
        vT_ready, vtr_ready, val_ready = sem("vT_ready"), sem("vtr_ready"), sem("val_ready")
        scr_written = sem("scr_written")
        st_loaded = [sem(f"st_loaded{n}") for n in range(2)]
        sm_ready, sm_done = sem("sm_ready"), sem("sm_done")
        mxT_ready, mx_ready, mxlo_ready = sem("mxT_ready"), sem("mx_ready"), sem("mxlo_ready")
        mx_loaded = [sem(f"mx_loaded{n}") for n in range(2)]
        st_ready, exp_done, prob_ready = sem("st_ready"), sem("exp_done"), sem("prob_ready")
        pv_ready, oT_ready = sem("pv_ready"), sem("oT_ready")
        otr_ready, rec_ready, onorm_ready = sem("otr_ready"), sem("rec_ready"), sem("onorm_ready")
        xadd_done = sem("xadd_done")
        out_done = sem("out_done")
        dve_passed, pe_passed = sem("dve_passed"), sem("pe_passed")
        pool_passed, sp_passed = sem("pool_passed"), sem("sp_passed")

        N_SCR, N_ST = 2, 6
        NG = NB * G

        def half_of(w, half):
            return w.rearrange("p (t n) -> p t n", n=F)[:, :, half * F // 2:(half + 1) * F // 2]

        block = ctx.enter_context(nc.Block())

        @block.sync
        def _(sp):
            def load_weights(m, w):
                for half in range(2):
                    sp.dma_start(w_raw[:, m, half * F:(half + 1) * F].rearrange("p (t n) -> p t n", n=w.shape[1]),
                                 w.rearrange("(a t p) n -> a p t n", a=2, p=P)[half]).then_inc(ld_w[m][half], 16)

            sp.dma_start(x[:, 0:TT, :], x_dram[:, 0:TT, :]).then_inc(ld_x0, 16)
            load_weights(0, w_up_t)
            load_weights(1, w_gate_t)
            load_weights(2, w_down_t)
            sp.dma_start(x[:, TT:2 * TT, :], x_dram[:, TT:2 * TT, :]).then_inc(ld_x1, 16)
            sp.dma_start(wqkv[:, :, :], w_qkv.rearrange("(t p) n -> p t n", p=P)).then_inc(ld_attn, 16)
            sp.dma_start(b_col[:, :], b_qkv).then_inc(ld_attn, 16)
            sp.dma_start(x[:, 2 * TT:NT, :], x_dram[:, 2 * TT:NT, :]).then_inc(ld_xr, 16)

            def x_parts(n, par):
                if not isinstance(n, int) or n > 1:
                    sp.wait_ge(g_ready, NE * (n - 1))
                    sp.sem_inc(sp_passed)
                for part, source, ready, done in ((xh, xnh, xnh_ready, xh_ready), (xl, xnl, xnl_ready, xl_ready)):
                    sp.wait_ge(ready, n)
                    sp.sem_inc(sp_passed)
                    sp.dma_start_transpose(part[:, par, :, :, :].rearrange("p t d q -> p (t d) q"),
                                           source[:, :, :].rearrange("p t d -> p (t d)")).then_inc(done, 16)

            def write_scratch(c, par):
                sp.wait_ge(qkv_lo, 3 * c + 3)
                sp.dma_start(k_scr[par].rearrange("a d g t -> (d g) a t"), k_hl[G * DH:P, :, :]).then_inc(scr_written, 16)
                sp.dma_start(q_scr[par].rearrange("a d h m t -> (d h) a m t"), q_hl[:, :, :, :]).then_inc(scr_written, 16)

            def read_scratch(c, par):
                sp.wait_ge(scr_written, 16 * N_SCR * (c + 1))
                for n in range(2):
                    rows = slice(2 * n * DH, (2 * n + 2) * DH)
                    sp.dma_start(q_st[rows, par, :, :],
                                 q_scr[par].rearrange("a d h m t -> (a d) (h m) t")).then_inc(st_loaded[par], 16)
                    for twice in range(2):
                        rows = slice((2 * n + twice) * DH, (2 * n + twice + 1) * DH)
                        sp.dma_start(k_st[rows, par, :, :], k_scr[par, n]).then_inc(st_loaded[par], 16)

            def load_max(b, k, half):
                par, seq = k // 2 % 2, k % 2
                sp.wait_ge(mxlo_ready, 2 * b + half + 1)
                heads, cols = slice(half * HH, (half + 1) * HH), slice(seq * S, (seq + 1) * S)
                for part in range(2):
                    sp.dma_start(q_st[64 + part:65 + part, par, heads, cols],
                                 mx_hl[:, half, part, :]).then_inc(mx_loaded[half], 16)

            def attention_pair(pair, last):
                c0 = 2 * pair
                for k in range(4):
                    b, odd = 2 * c0 + k, k % 2
                    c, par = c0 + k // 2, k // 2
                    for g in range(G):
                        if g in (0, 2) and not (last and k == 3):
                            load_max(b + 1, k + 1, g // 2)
                        if odd and g == 1 and not last:
                            write_scratch(c + 2, par)
                        if odd and g == 2 and not last:
                            sp.wait_ge(st_ready, 3 * G * (b + 1))
                            read_scratch(c + 2, par)
                        if last and k == 2 and g == 2:
                            x_parts(NC, 0)

            x_parts(1, 1)
            with sp.Fori(1, NC // 2) as i:
                x_parts(2 * i, 0)
                x_parts(2 * i + 1, 1)
            sp.wait_ge(const_ready, 3)
            write_scratch(0, 0)
            read_scratch(0, 0)
            load_max(0, 0, 0)
            write_scratch(1, 1)
            load_max(0, 0, 1)
            read_scratch(1, 1)
            with sp.Fori(0, NC // 2 - 1) as i:
                attention_pair(i, False)
            attention_pair(NC // 2 - 1, True)
            x_parts(NC + 1, 1)

            def store(t0, n):
                sp.wait_ge(res_done, 2 + NT + t0 + n)
                sp.dma_start(out_dram[:, bass.ds(t0, n), :], x[:, bass.ds(t0, n), :]).then_inc(out_done, 16)

            with sp.Fori(0, NC // 2 - 1) as i:
                for par in range(2):
                    x_parts(NC + 2 * i + par + 2, par)
                    store(TT * (2 * i + par), TT)
            store(TT * (NC - 2), TT)
            for t in range(TT):
                store(TT * (NC - 1) + t, 1)
            sp.wait_ge(out_done, 16 * (NC - 1 + TT))

        @block.gpsimd
        def _(pool):
            steps = [0]

            def step(ins):
                steps[0] += 1
                ins.then_inc(pool_self, 1)
                pool.wait_ge(pool_self, steps[0])

            step(pool.memset(ident32[:, :], 0.0))
            step(pool.affine_select(out=ident32[:, :], in_=ident32[:, :], compare_op=ALU.not_equal, fill=1.0,
                                    base=0, pattern=[[-1, P]], channel_multiplier=1))
            pool.memset(ones[:, :], 1.0).then_inc(const_ready, 1)
            pool.wait_ge(const_ready, 1)
            step(pool.memset(mask[:, :], 0.0))
            step(pool.affine_select(out=mask[:, P:S], in_=mask[:, P:S], compare_op=ALU.is_ge, fill=MASKED,
                                    base=0, pattern=[[-1, P]], channel_multiplier=1))
            step(pool.memset(val[:, :, :, :, :], 0.0))
            pool.memset(val[:, :, :, :, DH:DH + 1], 1.0).then_inc(const_ready, 1)
            pool.wait_ge(const_ready, 2)
            step(pool.memset(k_st[64:P, :, :, :], 0.0))
            step(pool.memset(k_st[64:66, :, :, :], MAX_UNIT))
            pool.memset(o_norm[:, :, :], 0.0).then_inc(xadd_done, 2)
            pool.wait_ge(xadd_done, 2)

            def causal(n, par):
                pool.wait_ge(exp_done, 3 * n + 3)
                pool.sem_inc(pool_passed)
                early = prob[:, par, 0:2, :].rearrange("p i (h q) -> p (i h) q", q=S)[:, :, 0:P]
                late = prob[:, par, 2, :].rearrange("p (h q) -> p h q", q=P)
                pool.affine_select(out=early, in_=early, compare_op=ALU.is_ge, fill=0.0, base=0,
                                   pattern=[[0, HPG], [1, P]], channel_multiplier=-1)
                pool.affine_select(out=late, in_=late, compare_op=ALU.is_ge, fill=0.0, base=0,
                                   pattern=[[0, HPG], [1, P]], channel_multiplier=-1).then_inc(prob_ready, 1)

            def max_rest(b, half):
                pool.wait_ge(mx_ready, 2 * b + half + 1)
                if not isinstance(b, int) or b > 0:
                    pool.wait_ge(mx_loaded[half], 32 * b)
                pool.tensor_tensor(mx_hl[:, half, 1, :], mx_32[:, half, :], mx_hl[:, half, 0, :],
                                   ALU.subtract).then_inc(mxlo_ready, 1)

            def attention_pair(pair, last):
                c0 = 2 * pair
                for k in range(4):
                    b, odd = 2 * c0 + k, k % 2
                    c = c0 + k // 2
                    for g in range(G):
                        end = last and k == 3
                        if odd and g in (2, 3):
                            add_output(b - 1, g - 2, 3 - g)
                        if not (end and g == 3):
                            causal(4 * b + g + 1, (g + 1) % 2)
                        if g in (0, 2) and not end:
                            max_rest(b + 1, g // 2)
                        if not odd and g == 3 and not last:
                            centre_chunk(NC + c + 3, (TT * (c + 3)) % NT, tr_ready, 2 * c + 8)
                        if odd and g == 2 and not last:
                            scale_chunk(NC + c + 3)
                    if last and k == 3:
                        normed_parts(NC + 1, 2 * NC + 1, TT, xnl_ready, NC)
                    if odd:
                        add_output(b, 0, 0)
                        add_output(b, 1, 1)

            def add_output(b, n, qt):
                pool.wait_ge(onorm_ready, 2 * b + n + 3)
                tile = x[:, 2 * b + qt, :]
                pool.tensor_tensor(tile, tile, o_norm[:, qt, :], ALU.add).then_inc(xadd_done, 1)

            def centre_chunk(q, t0, last_read, count):
                pool.wait_ge(ln_mv, q + 1)
                pool.wait_ge(last_read, count)
                pool.tensor_tensor(xn[:, :, :], x[:, bass.ds(t0, TT), :], mv[:, :, 0:1].to_broadcast([P, TT, D]),
                                   ALU.subtract).then_inc(xn_centred, 1)

            def scale_chunk(q):
                pool.wait_ge(ln_rstd, RSTD_STEPS * (q + 1))
                pool.wait_ge(xn_centred, q)
                pool.tensor_tensor(xn[:, :, :], xn[:, :, :], rstd[:, :].unsqueeze(2).to_broadcast([P, TT, D]),
                                   ALU.mult).then_inc(xn_ready, 1)

            def normed_chunk(q, t0, last_read, count):
                centre_chunk(q, t0, last_read, count)
                scale_chunk(q)

            def low_part(n, q):
                pool.wait_ge(xnh_ready, n)
                pool.wait_ge(xn_ready, q + 1)
                pool.wait_ge(xl_ready, 16 * n)
                pool.tensor_tensor(xnl[:, :, :], xn[:, :, :], xnh[:, :, :], ALU.subtract).then_inc(xnl_ready, 1)

            def normed_parts(n, q, t0, last_read, count):
                centre_chunk(q, t0, last_read, count)
                pool.wait_ge(ln_rstd, RSTD_STEPS * (q + 1))
                pool.wait_ge(xn_centred, q)
                pool.wait_ge(xh_ready, 16 * n)
                pool.tensor_tensor(xnh[:, :, :], xn[:, :, :], rstd[:, :].unsqueeze(2).to_broadcast([P, TT, D]),
                                   ALU.mult).then_inc(xnh_ready, 1)
                pool.wait_ge(xnh_ready, n)
                scale_chunk(q)
                low_part(n, q)

            for m in range(2):
                pool.wait_ge(thr_ready, m + 1)
                pool.tensor_scalar(w_neg[1 + m], half_of(w_raw[:, m, :], 1), w_thr[:, m, 1:2], None,
                                   ALU.is_lt).then_inc(neg_ready, 1)
            pool.wait_ge(thr_ready, 3)
            pool.tensor_scalar(down_neg[:, 0:F], w_raw[:, 2, 0:F], w_thr[:, 2, 1:2], None, ALU.is_lt).then_inc(neg_ready, 1)
            normed_parts(1, 1, TT, tr_ready, 2)
            pool.tensor_scalar(down_neg[:, F:2 * F], w_raw[:, 2, F:2 * F], w_thr[:, 2, 1:2], None,
                               ALU.is_lt).then_inc(neg_ready, 1)
            pool.tensor_scalar(down_pos, w_raw[:, 2, F:2 * F], w_thr[:, 2, 0:1], None, ALU.is_gt).then_inc(neg_ready, 1)
            pool.wait_ge(neg_ready, 5)
            pool.tensor_tensor(wT_down[:, NE // 2:NE, :].rearrange("p e n -> p (e n)"), down_pos, down_neg[:, F:2 * F],
                               ALU.subtract).then_inc(down_ready, 1)
            normed_parts(2, 2, 2 * TT, xnl_ready, 1)
            pool.wait_ge(xnl_ready, 2)
            pool.memset(q_st[64:P, :, :, :].bitcast(U32), 0).then_inc(const_ready, 1)
            pool.wait_ge(const_ready, 3)
            with pool.Fori(3, NC - 1) as c:
                normed_parts(c, c, TT * c, xnl_ready, c - 1)
            pool.wait_ge(most_ready, 1)
            pool.partition_all_reduce(qk_bound[:, :], qk_most[:, :], P, RMAX).then_inc(bound_ready, 1)
            normed_parts(NC - 1, NC - 1, TT * (NC - 1), xnl_ready, NC - 2)
            normed_chunk(NC, 0, xnl_ready, NC - 1)
            normed_chunk(NC + 1, TT, tr_ready, 4)
            centre_chunk(NC + 2, 2 * TT, tr_ready, 6)
            max_rest(0, 0)
            scale_chunk(NC + 2)
            max_rest(0, 1)
            causal(0, 0)
            with pool.Fori(0, NC // 2 - 1) as i:
                attention_pair(i, False)
            attention_pair(NC // 2 - 1, True)
            with pool.Fori(2, NC) as c:
                normed_parts(NC + c, 2 * NC + c, TT * c, xnl_ready, NC + c - 1)

        @block.scalar
        def _(act):
            def abs_sum(m, half):
                act.wait_ge(ld_w[m][half], 16)
                if m or half:
                    act.wait_ge(abs_ready, 2 * m + half)
                act.activation(w_abs[:, 0:F], w_raw[:, m, half * F:(half + 1) * F], ACT.Abs,
                               accum_out=w_sum[:, m, half:half + 1]).then_inc(abs_ready, 1)

            def first_x_high(d):
                act.wait_ge(tr_ready, d + 1)
                act.activation(xh[:, 0, :, d, :], TR[d][:, :].rearrange("p (t q) -> p t q", t=TT),
                               ACT.Copy).then_inc(xh_ready, 16 // ND)

            def feed_forward(ph):
                def chunk(c, par, beside=None):
                    for e in range(NE):
                        s = 64 * ph + NE * c + e
                        act.wait_ge(u_ready, s + 1)
                        if not (isinstance(s, int) and s < 2):
                            act.wait_ge(hid_ready, s - 1)
                        act.activation(silu[:, e % 2, :], U[e % 2][:, :], ACT.Silu,
                                       scale=w_scale[:, 0:1]).then_inc(silu_ready, 1)
                        if e:
                            hidden_high(s - 1, par, e - 1)
                        elif not (isinstance(c, int) and c == 0):
                            hidden_high(s - 1, 1 - par, NE - 1)
                        if beside:
                            beside(e)

                def hidden_high(s, par, e):
                    act.wait_ge(hid_ready, s + 1)
                    act.activation(hh[:, par, e, :], hid[:, e % 4, :], ACT.Copy).then_inc(hh_ready, 1)

                def attention_start(e):
                    if e == 0:
                        xT_copy(0)
                    if e == 2:
                        key_high(0)
                        values(0)
                    if e in (3, 4):
                        query_high(0, e - 3)
                    if e == 5:
                        val_copy(0, 0)

                chunk(0, 0)
                with act.Fori(0, NC // 2 - 1) as i:
                    chunk(2 * i + 1, 1)
                    chunk(2 * i + 2, 0)
                chunk(NC - 1, 1, None if ph else attention_start)
                hidden_high(64 * ph + 63, 1, NE - 1)

            def xT_copy(c, tiles=range(ND)):
                for d in tiles:
                    act.wait_ge(tr_ready, 2 * (c + 1) + d + 1)
                    act.activation(xT[:, d, :], MI[d][:, :], ACT.Copy).then_inc(xT_ready, 1)

            def key_high(c):
                act.wait_ge(qkv_ready, 3 * c + 1)
                if isinstance(c, int) and c == 0:
                    act.wait_ge(attn_w_ready, 3)
                else:
                    act.wait_ge(scr_written, 16 * N_SCR * c)
                act.activation(k_hl[G * DH:P, 0, :], MI[0][G * DH:P, :], ACT.Identity,
                               bias=b_col[G * DH:P, 0:1]).then_inc(qkv_hi, 1)

            def values(c):
                act.wait_ge(qkv_ready, 3 * c + 1)
                act.activation(vT[:, :], MI[0][0:G * DH, :], ACT.Identity, bias=b_col[0:G * DH, 0:1]).then_inc(vT_ready, 1)

            def query_high(c, m):
                act.wait_ge(qkv_ready, 3 * c + m + 2)
                act.activation(q_hl[:, 0, m, :], MI[1 - m][:, :], ACT.Identity,
                               bias=b_col[:, m + 1:m + 2]).then_inc(qkv_hi, 1)

            def val_copy(c, par):
                act.wait_ge(vtr_ready, c + 1)
                act.activation(val[:, par, :, :, 0:DH],
                               MI[1][:, 0:TT * G * DH].rearrange("p (t g d) -> p t g d", t=TT, g=G),
                               ACT.Copy).then_inc(val_ready, 1)

            def max_copy(b, half):
                act.wait_ge(mxT_ready, 2 * b + half + 1)
                if not (isinstance(b, int) and b == 0):
                    act.wait_ge(mx_loaded[half], 32 * b)
                maxima = FIRST_MT if isinstance(b, int) and b + half == 0 else MT
                act.activation(mx_hl[:, half, 0, :], maxima[0:HH, :], ACT.Copy, scale=-1.0 / MAX_UNIT)
                act.activation(mx_32[:, half, :], maxima[0:HH, :], ACT.Copy,
                               scale=-1.0 / MAX_UNIT).then_inc(mx_ready, 1)

            def exps(n, place, parts):
                for i in parts:
                    act.wait_ge(st_ready, 3 * n + i + 1)
                    act.activation(prob[:, place % 2, i, :], ST[(3 * place + i) % 2][:, :], ACT.Exp,
                                   scale=qk_scale[:, 4:5]).then_inc(exp_done, 1)

            def attention_pair(pair, last):
                c0 = 2 * pair
                for k in range(4):
                    b, odd = 2 * c0 + k, k % 2
                    c, par = c0 + k // 2, k // 2
                    for g in range(G):
                        n, end = 4 * b + g, last and k == 3
                        ahead = (n + 1, 4 * k + g + 1)
                        if not (end and g == 3):
                            exps(*ahead, range(0, 1))
                        if not last:
                            if not odd and g == 2:
                                key_high(c + 2)
                            if not odd and g == 3:
                                query_high(c + 2, 0)
                            if odd and g == 1:
                                query_high(c + 2, 1)
                        if not (end and g == 3):
                            exps(*ahead, range(1, 3))
                        if not odd and g == 0 and not last:
                            xT_copy(c + 2, range(0, 1))
                        if end and g == 3:
                            act.activation(silu[:, 1, 0:1], silu[:, 1, 0:1], ACT.Silu)
                        act.wait_ge(pv_ready, n + 1)
                        if g in (0, 2) and not end:
                            max_copy(b + 1, g // 2)
                        act.activation(oT[:, odd, g, :], PV[:, 0:S], ACT.Copy).then_inc(oT_ready, 1)
                        if odd and g == 3 and not last:
                            val_copy(c + 2, par)
                        if not odd and g == 0 and not last:
                            xT_copy(c + 2, range(1, 2))
                        if not odd and g == 2 and not last:
                            values(c + 2)

            def attention():
                xT_copy(1)
                act.activation(silu[:, 0, 0:1], silu[:, 0, 0:1], ACT.Exp)
                key_high(1)
                values(1)
                query_high(1, 0)
                max_copy(0, 0)
                query_high(1, 1)
                max_copy(0, 1)
                val_copy(1, 1)
                act.sem_inc(oT_ready)
                exps(0, 0, range(3))
                with act.Fori(0, NC // 2 - 1) as i:
                    attention_pair(i, False)
                attention_pair(NC // 2 - 1, True)

            for m in range(3):
                for half in range(2):
                    abs_sum(m, half)
                if m == 1:
                    for d in range(ND):
                        first_x_high(d)
            feed_forward(0)
            attention()
            feed_forward(1)

        @block.vector
        def _(dve):
            steps = [0]

            def step(ins):
                steps[0] += 1
                ins.then_inc(dve_self, 1)
                dve.wait_ge(dve_self, steps[0])

            def scale_of(m):
                dve.wait_ge(wsum_ready, m + 1)
                step(dve.tensor_scalar(w_scale[:, m:m + 1], ACC[m % 2][:, 0:1], 1.0 / (F * D), QUANT_EPS,
                                       ALU.mult, ALU.add))
                dve.tensor_scalar(w_thr[:, m, 0:1], w_scale[:, m:m + 1], 0.5, None, ALU.mult)
                step(dve.tensor_scalar(w_thr[:, m, 1:2], w_scale[:, m:m + 1], -0.5, None, ALU.mult))
                dve.sem_inc(thr_ready)

            def ternary(m, half):
                cols = slice(half * F // 2, (half + 1) * F // 2)
                raw, neg = half_of(w_raw[:, m, :], half), w_neg[1 + m if half else 0]
                if half:
                    dve.wait_ge(neg_ready, m + 1)
                else:
                    if m:
                        dve.wait_ge(tern_ready, 1)
                    step(dve.tensor_scalar(neg, raw, w_thr[:, m, 1:2], None, ALU.is_lt))
                dve.scalar_tensor_tensor(out=(wT_up, wT_gate)[m][:, :, cols], in0=raw, scalar=w_thr[:, m, 0:1],
                                         in1=neg, op0=ALU.is_gt, op1=ALU.subtract).then_inc(tern_ready, 1)

            def ternary_down():
                dve.wait_ge(neg_ready, 3)
                dve.scalar_tensor_tensor(out=wT_down[:, 0:NE // 2, :].rearrange("p e n -> p (e n)"), in0=w_raw[:, 2, 0:F], scalar=w_thr[:, 2, 0:1],
                                         in1=down_neg[:, 0:F], op0=ALU.is_gt, op1=ALU.subtract).then_inc(tern_ready, 1)

            def ln_stats_of(q, t0, tiles):
                for t in tiles:
                    ins = dve.bn_stats(stats[:, t, :], x[:, t0 + t, :])
                if TT - 1 in tiles:
                    ins.then_inc(ln_stats, 1)

            def ln_moments(q):
                dve.wait_ge(ln_stats, q + 1)
                if not (isinstance(q, int) and q == 0):
                    dve.wait_ge(xn_ready, q)
                dve.sem_inc(dve_passed)
                for t in range(TT):
                    ins = dve.bn_aggr(mv[:, t, :], stats[:, t, :])
                ins.then_inc(ln_mv, 1)

            def ln_rstd_steps(q, steps):
                for i in steps:
                    if i == 0:
                        dve.wait_ge(ln_mv, q + 1)
                        ins = dve.tensor_scalar(var[:, :], mv[:, :, 1], LN_EPS, None, ALU.add)
                    else:
                        dve.wait_ge(ln_rstd, RSTD_STEPS * q + i)
                    if i == 1:
                        ins = dve.tensor_scalar(rstd[:, :].bitcast(U32), var[:, :].bitcast(U32), 1, None,
                                                ALU.logical_shift_right)
                    elif i == 2:
                        ins = dve.tensor_scalar(rstd[:, :].bitcast(I32), rstd[:, :].bitcast(I32), -1.0,
                                                float(RSQRT_GUESS), ALU.mult, ALU.add)
                    elif i and i % 3 == 0:
                        ins = dve.tensor_tensor(newton[:, 0, :], var[:, :], rstd[:, :], ALU.mult)
                    elif i and i % 3 == 1:
                        ins = dve.scalar_tensor_tensor(out=newton[:, 1, :], in0=newton[:, 0, :], scalar=-0.5,
                                                       in1=rstd[:, :], op0=ALU.mult, op1=ALU.mult)
                    elif i:
                        ins = dve.scalar_tensor_tensor(out=rstd[:, :], in0=newton[:, 1, :], scalar=1.5,
                                                       in1=rstd[:, :], op0=ALU.add, op1=ALU.mult)
                    ins.then_inc(ln_rstd, 1)

            def ln_whole(q, t0):
                ln_stats_of(q, t0, range(TT))
                ln_moments(q)
                ln_rstd_steps(q, range(RSTD_STEPS))
                ln_4(q, t0)

            def ln_4(q, t0):
                dve.wait_ge(ln_rstd, RSTD_STEPS * (q + 1))
                for t in range(TT):
                    ins = dve.tensor_scalar(xn[:, t, :], x[:, t0 + t, :], mv[:, t, 0:1], rstd[:, t:t + 1],
                                            ALU.subtract, ALU.mult)
                ins.then_inc(xn_ready, 1)

            def first_x_low(d):
                dve.wait_ge(xh_ready, 16 // ND * (d + 1))
                dve.tensor_tensor(xl[:, 0, :, d, :], TR[d][:, :].rearrange("p (t q) -> p t q", t=TT), xh[:, 0, :, d, :],
                                  ALU.subtract).then_inc(xl_ready, 16 // ND)

            def feed_forward(ph):
                def chunk(c, par, down, norm, beside=None):
                    q = 2 * NC * ph + c + 1
                    first = isinstance(c, int) and c == 0
                    more = not first and (norm or (isinstance(c, int) and c == NC - 2))
                    for e in range(NE):
                        s = 64 * ph + NE * c + e
                        dve.wait_ge(silu_ready, s + 1)
                        dve.wait_ge(g_ready, s + 1)
                        if not (isinstance(s, int) and s < 4):
                            dve.wait_ge(hl_ready, s - 3)
                        dve.scalar_tensor_tensor(out=hid[:, e % 4, :], in0=silu[:, e % 2, :], scalar=h_unit[:, 0:1],
                                                 in1=GT[e % 2][:, :], op0=ALU.mult, op1=ALU.mult).then_inc(hid_ready, 1)
                        if e:
                            hidden_low(s - 1, par, e - 1)
                        elif not first:
                            hidden_low(s - 1, 1 - par, NE - 1)
                        if norm and e == 6:
                            if ph:
                                dve.wait_ge(xadd_done, 2 + TT * (c + 3))
                            else:
                                dve.wait_ge(ld_xr, 16)
                            ln_stats_of(q + 1, TT * (c + 2), range(0, 2))
                        if norm and e == 7:
                            ln_stats_of(q + 1, TT * (c + 2), range(2, 4))
                            ln_moments(q + 1)
                        if more and e < 2:
                            ln_rstd_steps(q, range(6 * e, 6 * e + 6))
                        if beside:
                            beside(e)
                        if down and e % 2:
                            residual(c - 1, e // 2)

                def hidden_low(s, par, e):
                    dve.wait_ge(hh_ready, s + 1)
                    dve.tensor_tensor(hl[:, par, e, :], hid[:, e % 4, :], hh[:, par, e, :],
                                      ALU.subtract).then_inc(hl_ready, 1)

                def residual(c, t):
                    dve.wait_ge(acc_ready, NT * ph + TT * c + t + 1)
                    tile = x[:, TT * c + t, :]
                    dve.scalar_tensor_tensor(out=tile, in0=ACC[t % 2][:, 0:D], scalar=y_scale[:, 1:2], in1=tile,
                                             op0=ALU.mult, op1=ALU.add).then_inc(res_done, 1)

                def start(e):
                    if e == 0:
                        ln_rstd_steps(1, range(RSTD_STEPS))
                    if e < 2:
                        ternary(e, 1)
                    if e == 4:
                        ternary_down()
                    if e == 2:
                        step(dve.tensor_tensor(y_scale[:, 0:1], w_scale[:, 0:1], w_scale[:, 1:2], ALU.mult))
                        step(dve.tensor_tensor(y_scale[:, 1:2], y_scale[:, 0:1], w_scale[:, 2:3], ALU.mult))

                def next_norm(e):
                    if e == 2:
                        dve.wait_ge(res_done, 2 + TT)
                        ln_stats_of(NC, 0, range(TT))
                    if e == 3:
                        ln_moments(NC)
                    if e in (4, 5):
                        ln_rstd_steps(NC, range(6 * e - 24, 6 * e - 18))
                    if e == 6:
                        projection_scales()
                    if e == 7:
                        scale_projections()

                def attention_start(e):
                    if e < 2:
                        dve.wait_ge(res_done, 2 + 2 * TT)
                        ln_stats_of(NC + 1, TT, range(2 * e, 2 * e + 2))
                    if e == 1:
                        ln_moments(NC + 1)
                    if e == 2:
                        key_low(0)
                    if e in (3, 4):
                        query_low(0, e - 3)
                    if e in (2, 3, 4, 5):
                        ln_rstd_steps(NC + 1, range(3 * e - 6, 3 * e - 3))
                    if e in (6, 7):
                        dve.wait_ge(res_done, 2 + 3 * TT)
                        ln_stats_of(NC + 2, 2 * TT, range(2 * e - 12, 2 * e - 10))
                    if e == 7:
                        ln_moments(NC + 2)

                chunk(0, 0, False, True, None if ph else start)
                with dve.Fori(0, NC // 2 - 2) as i:
                    chunk(2 * i + 1, 1, True, True)
                    chunk(2 * i + 2, 0, True, True)
                chunk(NC - 3, 1, True, True, None if ph else projection_ends)
                chunk(NC - 2, 0, True, False, None if ph else next_norm)
                chunk(NC - 1, 1, True, False, None if ph else attention_start)
                hidden_low(64 * ph + 63, 1, NE - 1)
                for t in range(TT):
                    if ph == 0 and t < 3:
                        first_row_max(t)
                    residual(NC - 1, t)
                    if ph == 0:
                        if t == 2:
                            first_row_max(3)
                        if t == 0:
                            key_low(1)
                        elif t < 3:
                            query_low(1, t - 1)

            def projection_ends(e):
                if e == 3:
                    dve.wait_ge(ld_attn, 16 * 2)
                    step(dve.memset(qk_ends[:, :, :], 0.0))
                if e in (4, 5):
                    n, op = e - 4, (ALU.max, ALU.min)[e - 4]
                    dve.tensor_reduce(qk_ends[:, n, 0:1], wqkv[:, :, P:3 * P], mybir.AxisListType.XY, op)
                    dve.tensor_reduce(qk_ends[:, n, 1:2], wqkv[:, :, G * DH:P], mybir.AxisListType.XY, op)
                    dve.tensor_reduce(qk_ends[:, n, 2:3], b_col[:, 1:3], AXX, op)
                    step(dve.tensor_copy(qk_ends[G * DH:P, n, 3:4], b_col[G * DH:P, 0:1]))
                if e == 5:
                    dve.scalar_tensor_tensor(out=qk_most[:, :], in0=qk_ends[:, 1, :], scalar=-1.0, in1=qk_ends[:, 0, :],
                                             op0=ALU.mult, op1=ALU.max).then_inc(most_ready, 1)

            def projection_scales():
                dve.wait_ge(bound_ready, 1)
                step(dve.scalar_tensor_tensor(out=qk_scale[:, 0:2], in0=qk_bound[:, 0:2], scalar=float(D),
                                              in1=qk_bound[:, 2:4], op0=ALU.mult, op1=ALU.add))
                step(dve.tensor_scalar(qk_scale[:, 0:2], qk_scale[:, 0:2], 1e-12, None, ALU.max))
                step(dve.reciprocal(qk_scale[:, 2:4], qk_scale[:, 0:2]))
                step(dve.tensor_scalar(qk_scale[:, 2:4].bitcast(U32), qk_scale[:, 2:4].bitcast(U32), EXPONENT_BITS, None,
                                       ALU.bitwise_and))
                step(dve.tensor_scalar(qk_scale[:, 2:4], qk_scale[:, 2:4], QK_BOUND, None, ALU.mult))
                step(dve.tensor_tensor(qk_scale[:, 5:6], qk_scale[:, 2:3], qk_scale[:, 3:4], ALU.mult))
                step(dve.reciprocal(qk_scale[:, 6:7], qk_scale[:, 5:6]))
                dve.tensor_scalar(qk_scale[:, 4:5], qk_scale[:, 6:7], float(DH) ** -0.5, None,
                                  ALU.mult).then_inc(attn_w_ready, 1)

            def scale_projections():
                dve.wait_ge(attn_w_ready, 1)
                dve.tensor_scalar(wqkv[:, :, P:3 * P], wqkv[:, :, P:3 * P], qk_scale[:, 2:3], None, ALU.mult)
                dve.tensor_scalar(wqkv[:, :, G * DH:P], wqkv[:, :, G * DH:P], qk_scale[:, 3:4], None,
                                  ALU.mult).then_inc(attn_w_ready, 1)
                dve.tensor_scalar(b_col[:, 1:3], b_col[:, 1:3], qk_scale[:, 2:3], None, ALU.mult)
                dve.tensor_scalar(b_col[G * DH:P, 0:1], b_col[G * DH:P, 0:1], qk_scale[G * DH:P, 3:4], None,
                                  ALU.mult).then_inc(attn_w_ready, 1)

            def key_low(c):
                dve.wait_ge(qkv_hi, 3 * c + 1)
                dve.scalar_tensor_tensor(out=k_hl[G * DH:P, 1, :], in0=MI[0][G * DH:P, :], scalar=b_col[G * DH:P, 0:1],
                                         in1=k_hl[G * DH:P, 0, :], op0=ALU.add, op1=ALU.subtract).then_inc(qkv_lo, 1)

            def query_low(c, m):
                dve.wait_ge(qkv_hi, 3 * c + m + 2)
                dve.scalar_tensor_tensor(out=q_hl[:, 1, m, :], in0=MI[1 - m][:, :], scalar=b_col[:, m + 1:m + 2],
                                         in1=q_hl[:, 0, m, :], op0=ALU.add, op1=ALU.subtract).then_inc(qkv_lo, 1)

            def row_max(n, seq_par, g, i, norm, steps):
                dve.wait_ge(sm_ready, 3 * n + i + 1)
                dve.sem_inc(dve_passed)
                heads = range(HPG) if i == 2 else range(2 * i, 2 * i + 2)
                size, qt = (P, 0) if i == 2 else (S, 1)
                for j in heads:
                    cols = slice((j - heads[0]) * size, (j - heads[0] + 1) * size)
                    h = HPG * g + j
                    ins = dve.tensor_tensor_reduce(sm_out[:, i, cols], SM[i][:, cols], mask[:, S - size:S], 1.0, MASKED,
                                                   ALU.add, ALU.max, rowmax[:, seq_par, qt, h:h + 1])
                    if j == heads[-1]:
                        ins.then_inc(sm_done, 1)
                    else:
                        at = j // 2 if i < 2 else j // 2 + 2
                        if i < 2 or j != 1:
                            ln_rstd_steps(norm, steps[at:at + 1])

            def normalise(b, n, qt):
                heads = MI[qt][:, :].rearrange("p (h w) -> p h w", w=VW)
                dve.wait_ge(otr_ready, 2 * b + n + 1)
                dve.reciprocal(o_rec[:, qt, :], heads[:, :, DH]).then_inc(rec_ready, 1)
                dve.wait_ge(rec_ready, 2 * b + n + 1)
                dve.wait_ge(xadd_done, 2 * b + 2 - n)
                dve.tensor_tensor(o_norm[:, qt, :].rearrange("p (h d) -> p h d", d=DH), heads[:, :, 0:DH],
                                  o_rec[:, qt, :].unsqueeze(2).to_broadcast([P, H, DH]),
                                  ALU.mult).then_inc(onorm_ready, 1)

            def first_parts():
                dve.wait_ge(xn_ready, 2 * NC + 1)
                dve.wait_ge(xh_ready, 16 * NC)
                dve.tensor_copy(xnh[:, :, :], xn[:, :, :]).then_inc(xnh_ready, 1)
                dve.wait_ge(xl_ready, 16 * NC)
                dve.wait_ge(xnh_ready, NC)
                dve.tensor_tensor(xnl[:, :, :], xn[:, :, :], xnh[:, :, :], ALU.subtract).then_inc(xnl_ready, 1)

            def attention_pair(pair, last):
                c0 = 2 * pair
                for k in range(4):
                    b, odd = 2 * c0 + k, k % 2
                    c = c0 + k // 2
                    q = NC + c + 3
                    for g in range(G):
                        lead = (4 * b + g + 6, (k + (g + 6) // 4) % 2, (g + 2) % 4)
                        ahead = not (last and (k == 3 or (k == 2 and g >= 2)))
                        norm = () if last else {(0, 3): range(0, 4), (1, 0): range(4, 8),
                                                (1, 1): range(8, 12)}.get((odd, g), ())
                        for i in range(3):
                            if ahead and not (not odd and g == 0 and i == 0):
                                row_max(*lead, i, q, norm)
                            if not odd and not last:
                                if g == 1 and i == 0:
                                    dve.wait_ge(xadd_done, TT * c + 1)
                                if g == 1 or (g == 2 and i == 0):
                                    t = i if g == 1 else 3
                                    ln_stats_of(q, (TT * (c + 3)) % NT, range(t, t + 1))
                                if g == 2 and i == 1:
                                    ln_moments(q)
                                if g == 2 and i == 2:
                                    key_low(c + 2)
                                if g == 3 and i == 2:
                                    query_low(c + 2, 0)
                            if odd and g == 1 and i == 2 and not last:
                                query_low(c + 2, 1)
                            if last and k == 3 and i == 1:
                                if g == 0:
                                    dve.wait_ge(xadd_done, 2 + 2 * TT)
                                    ln_stats_of(2 * NC + 1, TT, range(TT))
                                if g == 1:
                                    ln_moments(2 * NC + 1)
                                if g == 2:
                                    ln_rstd_steps(2 * NC + 1, range(RSTD_STEPS))
                            if last and k == 2 and g == 1 and i == 0:
                                first_parts()
                            if odd and g in (1, 3) and i == 0:
                                normalise(b - 1, g // 2, 1 - g // 2)
                    if odd:
                        if not (last and k == 3):
                            row_max(4 * b + 10, (k + 2) % 2, 2, 0, q, ())
                        normalise(b, 0, 0)
                        normalise(b, 1, 1)

            def first_row_max(n):
                if n == 0:
                    dve.wait_ge(const_ready, 2)
                for i in range(3):
                    row_max(n, n // G, n % G, i, NC + 2, range(4 * n, 4 * n + 4) if n < 3 else ())

            def attention():
                for n in (4, 5):
                    first_row_max(n)
                row_max(6, 1, 2, 0, NC + 2, ())
                dve.wait_ge(val_ready, 2)
                dve.memset(o_rec[:, 0, 0:1], 0.0).then_inc(onorm_ready, 2)
                with dve.Fori(0, NC // 2 - 1) as i:
                    attention_pair(i, False)
                attention_pair(NC // 2 - 1, True)

            dve.wait_ge(ld_x0, 16)
            ln_whole(0, 0)
            scale_of(0)
            ternary(0, 0)
            for d in range(ND):
                first_x_low(d)
            scale_of(1)
            ternary(1, 0)
            step(dve.reciprocal(h_unit[:, 1:2], w_scale[:, 0:1]))
            step(dve.tensor_scalar(h_unit[:, 0:1], h_unit[:, 1:2], 0.5, None, ALU.mult))
            scale_of(2)
            dve.wait_ge(ld_x1, 16)
            ln_stats_of(1, TT, range(TT))
            ln_moments(1)
            dve.memset(newton[:, :, :], 0.0).then_inc(res_done, 2)
            feed_forward(0)
            attention()
            feed_forward(1)

        @block.tensor
        def _(pe):
            def weight_sum(m):
                pe.wait_ge(abs_ready, 2 * m + 2)
                if m == 2:
                    pe.wait_ge(tern_ready, 1)
                for half in range(2):
                    ins = pe.matmul(ACC[m % 2][:, 0:1], ones[:, :], w_sum[:, m, half:half + 1],
                                    start=(half == 0), stop=(half == 1))
                ins.then_inc(wsum_ready, 1)

            def x_transposes(q, ready):
                pe.wait_ge(xn_ready, q + 1)
                for d in range(ND):
                    for ready_sem, count in ready[d]:
                        pe.wait_ge(ready_sem, count)
                    for t in range(TT):
                        ins = pe.transpose(TR[d][:, t * P:(t + 1) * P], xn[:, t, d * P:(d + 1) * P], ident32[:, :])
                    ins.then_inc(tr_ready, 1)

            def up_or_gate(s, e, par, gate):
                w, banks, done = (wT_gate, GT, g_ready) if gate else (wT_up, U, u_ready)
                if not (isinstance(s, int) and s < 2):
                    pe.wait_ge(hid_ready if gate else silu_ready, s - 1)
                for d in range(ND):
                    for part in (xh, xl):
                        ins = pe.matmul(banks[e % 2][:, :], w[:, d, e * P:(e + 1) * P], part[:, par, :, d, :],
                                        start=(d == 0 and part is xh), stop=(d == ND - 1 and part is xl))
                ins.then_inc(done, 1)

            def feed_forward(ph):
                def down_half(c, par, t, half):
                    n = NT * ph + TT * c + t
                    if half == 0:
                        pe.wait_ge(res_done, n + 1)
                    for e in range(half * 4, half * 4 + 4):
                        for part in (hh, hl):
                            ins = pe.matmul(ACC[t % 2][:, 0:D], part[:, par, e, t * P:(t + 1) * P], wT_down[:, e, :],
                                            start=(e == 0 and part is hh), stop=(e == NE - 1 and part is hl))
                    if half:
                        ins.then_inc(acc_ready, 1)

                def chunk(c, par, down, beside=None):
                    n = NC * ph + c
                    first = isinstance(c, int) and c == 0
                    pe.wait_ge(xh_ready, 16 * (n + 1))
                    pe.wait_ge(xl_ready, 16 * (n + 1))
                    for e in range(NE):
                        s = 64 * ph + NE * c + e
                        for gate in range(2):
                            if ph == 0 and first and e % 4 == 0:
                                pe.wait_ge(tern_ready, 1 + e // 2 + gate)
                            if not (ph and first and e == 0):
                                up_or_gate(s, e, par, gate)
                            if ph == 0 and first and e + gate == 0:
                                weight_sum(2)
                        if down:
                            if e < 2:
                                pe.wait_ge(hl_ready, s - 4 + 3 * e)
                            if ph == 0 and not isinstance(c, int) and e < 2:
                                pe.wait_ge(*((tern_ready, 5), (down_ready, 1))[e])
                            down_half(c - 1, 1 - par, e // 2, e % 2)
                        if beside:
                            beside(e)

                def next_norm(e):
                    if e == 7:
                        x_transposes(NC, [[], []])

                def attention_start(e):
                    if e == 1:
                        project_all(0, 0)
                    if e in (2, 3):
                        project_all(0, e - 1)
                    if e == 4:
                        val_transposes(0, (qkv_lo, 2))
                    if e == 7:
                        x_transposes(NC + 1, [[(qkv_lo, 3)], [(val_ready, 1)]])

                chunk(0, 0, False)
                with pe.Fori(0, NC // 2 - 2) as i:
                    chunk(2 * i + 1, 1, True)
                    chunk(2 * i + 2, 0, True)
                chunk(NC - 3, 1, True)
                chunk(NC - 2, 0, True, None if ph else next_norm)
                chunk(NC - 1, 1, True, None if ph else attention_start)
                pe.wait_ge(hl_ready, 64 * (ph + 1) - 4)
                down_half(NC - 1, 1, 0, 0)
                down_half(NC - 1, 1, 1, 0)
                pe.wait_ge(hl_ready, 64 * (ph + 1))
                for t in range(TT):
                    if ph == 0:
                        if t == 0:
                            pe.wait_ge(st_loaded[0], 16 * N_ST)
                        if t < 3:
                            max_scores(t, 0, t)
                    if t > 1:
                        down_half(NC - 1, 1, t, 0)
                    down_half(NC - 1, 1, t, 1)
                    if ph == 0:
                        if t == 2:
                            max_transposes(0, 0, 0)
                            max_scores(3, 0, 3)
                        if t < 3:
                            project_all(1, t)

            def project(c, m, part):
                half, d = part // ND, part % ND
                cols = slice(half * S, (half + 1) * S)
                if m == 0 and part < ND:
                    if isinstance(c, int) and c == 0:
                        pe.wait_ge(attn_w_ready, 3)
                    pe.wait_ge(xT_ready, 2 * c + 1 + part)
                if m == 2 and part == 0:
                    pe.wait_ge(vT_ready, c + 1)
                    pe.wait_ge(qkv_lo, 3 * c + 1)
                ins = pe.matmul(MI[m % 2][:, cols], wqkv[:, d, m * P:(m + 1) * P], xT[:, d, cols], start=(d == 0), stop=(d == ND - 1))
                if part == 2 * ND - 1:
                    ins.then_inc(qkv_ready, 1)

            def project_all(c, m):
                for part in range(2 * ND):
                    project(c, m, part)

            def val_transposes(c, last_reader):
                pe.wait_ge(vT_ready, c + 1)
                pe.wait_ge(*last_reader)
                pe.sem_inc(pe_passed)
                for t in range(TT):
                    ins = pe.transpose(MI[1][:, t * G * DH:(t + 1) * G * DH], vT[:, t * P:(t + 1) * P],
                                       ident32[0:G * DH, 0:G * DH])
                ins.then_inc(vtr_ready, 1)

            def max_scores(n, k, g, parts=range(3)):
                par, at = k // 2 % 2, k % 2 * S
                for i in parts:
                    if not (isinstance(n, int) and n == 0):
                        pe.wait_ge(sm_done, 3 * n + i - 2)
                    heads = range(HPG) if i == 2 else range(2 * i, 2 * i + 2)
                    size, rows = (P, at) if i == 2 else (S, at + P)
                    for j in heads:
                        ins = pe.matmul(SM[i][:, (j - heads[0]) * size:(j - heads[0] + 1) * size],
                                        q_st[0:4 * DH, par, HPG * g + j, rows:rows + P],
                                        k_st[0:4 * DH, par, g, at:at + size],
                                        start=True, stop=True)
                    ins.then_inc(sm_ready, 1)

            def max_transposes(b, k, half):
                pe.wait_ge(sm_done, 3 * (G * b + 2 * half + 2))
                if not (isinstance(b, int) and b == 0 and half == 0):
                    pe.wait_ge(mx_ready, 2 * b + half)
                for qt in range(QT):
                    ins = pe.transpose((FIRST_MT if isinstance(b, int) and b + half == 0 else MT)[0:HH, qt * P:(qt + 1) * P], rowmax[:, k % 2, qt, half * HH:(half + 1) * HH],
                                       ident32[:, :])
                ins.then_inc(mxT_ready, 1)

            def scores(n, b, k, g, parts=range(3)):
                par, seq = k // 2 % 2, k % 2
                if g % 2 == 0 and 0 in parts:
                    pe.wait_ge(mx_loaded[g // 2], 32 * (b + 1))
                at, heads = seq * S, slice(HPG * g, HPG * (g + 1))
                for i in parts:
                    if not (isinstance(n, int) and n == 0 and i < 2):
                        pe.wait_ge(exp_done, 3 * n + i - 1)
                    if i < 2:
                        keys, queries = at, q_st[:, par, HPG * g + 2 * i:HPG * g + 2 * i + 2, at:at + S]
                    else:
                        keys, queries = at + P, q_st[:, par, heads, at + P:at + S]
                    pe.matmul(ST[(3 * (4 * k + g) + i) % 2][:, :], k_st[:, par, g, keys:keys + P], queries,
                              start=True, stop=True).then_inc(st_ready, 1)

            def outputs(n, k, g):
                par, seq = k // 2 % 2, k % 2
                pe.wait_ge(prob_ready, n + 1)
                for j in range(HPG):
                    rows = slice(VW * j, VW * (j + 1))
                    pe.matmul(PV[rows, 0:S], val[:, par, QT * seq, g, :],
                              prob[:, g % 2, j // 2, (j % 2) * S:(j % 2 + 1) * S], start=True, stop=False,
                              tile_position=(0, VW * j))
                for j in range(HPG):
                    rows = slice(VW * j, VW * (j + 1))
                    ins = pe.matmul(PV[rows, P:S], val[:, par, QT * seq + 1, g, :],
                                    prob[:, g % 2, 2, j * P:(j + 1) * P], start=False, stop=True,
                                    tile_position=(0, VW * j))
                ins.then_inc(pv_ready, 1)

            def output_transposes(b, k, qt, last_reader):
                pe.wait_ge(oT_ready, G * (b + 1) + 1)
                pe.wait_ge(*last_reader)
                for g in range(G):
                    ins = pe.transpose(MI[qt][:, g * P:(g + 1) * P], oT[:, k % 2, g, qt * P:(qt + 1) * P], ident32[:, :])
                ins.then_inc(otr_ready, 1)

            PLACES = [(1, 1), (1, 2), (1, 3), (2, 0), (2, 1), (2, 2), (3, 0), (3, 1), (3, 2), (4, 0), (4, 2), (5, 0)]

            def attention_pair(pair, last):
                c0 = 2 * pair
                for k in range(4):
                    b, odd = 2 * c0 + k, k % 2
                    c, par = c0 + k // 2, k // 2
                    for g in range(G):
                        n, end = 4 * b + g, last and k == 3
                        lead = (n + 6, k + (g + 6) // 4, (g + 2) % 4)
                        ahead = not (end or (last and k == 2 and g >= 2))
                        def projection(place):
                            if (4 * odd + g, place) in PLACES and not last:
                                at = PLACES.index((4 * odd + g, place))
                                project(c + 2, at // 4, at % 4)

                        following = (n + 1, b + (g + 1) // 4, k + (g + 1) // 4, (g + 1) % 4)
                        if ahead:
                            if not odd and g == 2:
                                pe.wait_ge(st_loaded[1 - par], 16 * N_ST * (pair + par + 1))
                            if odd or g:
                                max_scores(*lead, range(0, 1))
                        projection(0)
                        if not (end and g == 3):
                            scores(*following, range(0, 1))
                        if ahead:
                            max_scores(*lead, range(1, 2))
                        projection(1)
                        if not (end and g == 3):
                            scores(*following, range(1, 2))
                        if ahead:
                            max_scores(*lead, range(2, 3))
                        projection(2)
                        if not odd and g == 0 and not last:
                            x_transposes(NC + c + 2, [[(onorm_ready, 2 * b + 1)], [(onorm_ready, 2 * b + 2)]])
                        if odd and g in (0, 2):
                            i = g // 2
                            output_transposes(b - 1, k - 1, 1 - i, (qkv_lo, 3 * (c + 2) + 2 + i) if not last else
                                              (onorm_ready, 2 * b - i))
                        if not (end and g == 3):
                            scores(*following, range(2, 3))
                        if end and g > 1:
                            if g == 2:
                                pe.wait_ge(xh_ready, 16 * (NC + 1))
                                pe.wait_ge(xl_ready, 16 * (NC + 1))
                            up_or_gate(64, 0, 0, g == 3)
                        if g == 0 and not odd:
                            pe.wait_ge(val_ready, c + 1)
                        pe.wait_ge(oT_ready, n + 1)
                        if g in (0, 2) and not end:
                            max_transposes(b + 1, k + 1, g // 2)
                        outputs(n, k, g)
                        if odd and g == 3 and not last:
                            val_transposes(c + 2, (onorm_ready, 2 * b + 1))
                        projection(3)
                        if odd and g == 3:
                            if not end:
                                max_scores(n + 7, k + 2, 2, range(0, 1))
                            output_transposes(b, k, 0, (onorm_ready, 2 * b + 2))
                            output_transposes(b, k, 1, (onorm_ready, 2 * b + 1) if last else (val_ready, c + 3))

            def attention():
                max_scores(4, 1, 0)
                pe.wait_ge(res_done, NT + 2)
                max_transposes(0, 0, 1)
                val_transposes(1, (qkv_lo, 5))
                scores(0, 0, 0, 0)
                max_scores(5, 1, 1)
                max_scores(6, 1, 2, range(0, 1))
                pe.wait_ge(val_ready, 2)
                with pe.Fori(0, NC // 2 - 1) as i:
                    attention_pair(i, False)
                attention_pair(NC // 2 - 1, True)

            pe.wait_ge(const_ready, 1)
            weight_sum(0)
            x_transposes(0, [[], []])
            weight_sum(1)
            feed_forward(0)
            attention()
            feed_forward(1)


def kernel(L0_attn_x, L0_attn_Wq, L0_attn_bq, L0_attn_Wk, L0_attn_bk, L0_attn_Wv, L0_attn_bv,
           L0_ffn_W_up, L0_ffn_W_gate, L0_ffn_W_down):
    import numpy as _np
    import concourse.bacc as _bacc
    from concourse import mybir as _mybir
    from concourse.bass_utils import run_bass_kernel_spmd as _run

    x = _np.asarray(L0_attn_x)
    wq, wk, wv = _np.asarray(L0_attn_Wq), _np.asarray(L0_attn_Wk), _np.asarray(L0_attn_Wv)
    bq, bk, bv = _np.asarray(L0_attn_bq), _np.asarray(L0_attn_bk), _np.asarray(L0_attn_bv)
    (h, e, d), g = wq.shape, wk.shape[0]
    w_qkv = _np.concatenate([wv.transpose(1, 0, 2).reshape(e, g * d), wk.transpose(1, 2, 0).reshape(e, g * d),
                             wq[0::2].transpose(1, 2, 0).reshape(e, h * d // 2),
                             wq[1::2].transpose(1, 2, 0).reshape(e, h * d // 2)], axis=1)
    b_qkv = _np.stack([_np.concatenate([bv.reshape(-1), bk.T.reshape(-1)]),
                       bq[0::2].T.reshape(-1), bq[1::2].T.reshape(-1)], axis=1)
    laid = {"x": x, "w_qkv": w_qkv, "b_qkv": b_qkv, "w_up_t": _np.asarray(L0_ffn_W_up).T,
            "w_gate_t": _np.asarray(L0_ffn_W_gate).T, "w_down_t": _np.asarray(L0_ffn_W_down).T}

    nc = _bacc.Bacc("TRN2", target_bir_lowering=False, num_devices=1)
    arrays, args = {}, []
    for name, a in laid.items():
        a = _np.ascontiguousarray(a)
        arrays[f"in_{name}_dram"] = a
        args.append(nc.dram_tensor(f"in_{name}_dram", a.shape, _mybir.dt.from_np(a.dtype), kind="ExternalInput").ap())
    out = nc.dram_tensor("out_0_dram", x.shape, _mybir.dt.from_np(x.dtype), kind="ExternalOutput").ap()
    macaron_block(nc, (h, g, d), *args, out)
    r = _run(nc, [arrays], core_ids=[0])
    return r.results[0]["out_0_dram"]
```
